# Optimizing a Trainium2 kernel written in Bass

```python
import numpy as np
import jax
import jax.numpy as jnp

def _softmax(x, axis=-1):
    return jax.nn.softmax(x, axis=axis)

def _gelu(x):
    return jax.nn.gelu(x, approximate=True)

def _silu(x):
    return jax.nn.silu(x)

def _sigmoid(x):
    return jax.nn.sigmoid(x)

def _layernorm(x, axis=-1, eps=1e-05):
    m = jnp.mean(x, axis=axis, keepdims=True)
    v = jnp.var(x, axis=axis, keepdims=True)
    return (x - m) / jnp.sqrt(v + eps)

def _scatter_add(tgt, idx, src, axis=0):
    return tgt.at[idx].add(src)

def _segment_sum(src, seg, n):
    return jax.ops.segment_sum(src, seg, n)
kernel_name = 'mk_decoder_postln_d1_seqx_r4_22a567'

def setup_inputs(seed: int=0):
    np.random.seed(seed)
    _w = jnp.asarray

    def _rec_inputs():
        import jax
        import jax.numpy as jnp
        _rk = jax.random.key(seed)
        x = -0.000125 + 0.9999 * jax.random.normal(jax.random.fold_in(_rk, 1), (4, 512, 512), jnp.float32)
        _lenS = 512 - jax.random.randint(jax.random.fold_in(_rk, 7), (4,), 0, max(1, 512 // 4) + 1, jnp.int32)
        _lenS2 = 512 - jax.random.randint(jax.random.fold_in(_rk, 8), (4,), 0, max(1, 512 // 4) + 1, jnp.int32)
        itok_BxS_13_99985 = jax.random.randint(jax.random.fold_in(_rk, 11), (4, 512), 13, 99986, jnp.int32)
        _ctx_2048P = jax.random.normal(jax.random.fold_in(_rk, 12), (4, 16, 512), jnp.float32)
        _ctx_2048c = jax.random.dirichlet(jax.random.fold_in(_rk, 512), 0.3 * jnp.ones((16,), jnp.float32), (4, 512))
        _ctx_2048t = jnp.einsum('bsk,bkd->bsd', _ctx_2048c, _ctx_2048P)
        _ctx_2048t = _ctx_2048t * jax.lax.rsqrt(jnp.mean(jnp.square(_ctx_2048t)) + 1e-12) * 0.953939
        ctx_2048 = 6.82029e-06 + 0.0200006 * (_ctx_2048t + 0.3 * jax.random.normal(jax.random.fold_in(_rk, 612), (4, 512, 512), jnp.float32))
        return (x, itok_BxS_13_99985, ctx_2048)
    x, itok_BxS_13_99985, ctx_2048 = _rec_inputs()

    def _L0_attn_setup():
        import jax, jax.numpy as jnp
        import numpy as np
        N_HEAD = 16
        key = jax.random.key(seed)
        k1, k2, k3 = jax.random.split(key, 3)
        B, T, C = (4, 256, 512)
        x = jax.random.normal(k1, (B, T, C), dtype=jnp.float32)
        w_attn = jax.random.normal(k2, (C, 3 * C), dtype=jnp.float32) * (1.0 / np.sqrt(C))
        b_attn = jnp.zeros((3 * C,), dtype=jnp.float32)
        w_proj = jax.random.normal(k3, (C, C), dtype=jnp.float32) * (1.0 / np.sqrt(C))
        b_proj = jnp.zeros((C,), dtype=jnp.float32)
        return {'x': x, 'w_attn': w_attn, 'b_attn': b_attn, 'w_proj': w_proj, 'b_proj': b_proj}
    _L0_attn_all = _L0_attn_setup()
    _L0_attn_in = {k: v for k, v in _L0_attn_all.items() if k in ('w_attn', 'b_attn', 'w_proj', 'b_proj')}
    del _L0_attn_all

    def _L0_xattn_setup():
        import jax, jax.numpy as jnp
        import numpy as np
        B, S, D = (4, 1024, 512)
        E = 4
        F = 2048 // E
        VOCAB = 25000
        key = jax.random.key(seed)
        k1, k2, k3, k4, k5 = jax.random.split(key, 5)
        hidden_states = jax.random.normal(k1, (B, S, D), dtype=jnp.float32)
        token_ids = jax.random.randint(k2, (B, S), 0, VOCAB, dtype=jnp.int64)
        Wg = jax.random.normal(k3, (E, F, D), dtype=jnp.float32) * 0.02
        Wu = jax.random.normal(k4, (E, F, D), dtype=jnp.float32) * 0.02
        Wd = jax.random.normal(k5, (E, D, F), dtype=jnp.float32) * 0.02
        return {'hidden_states': hidden_states, 'token_ids': token_ids, 'Wg': Wg, 'Wu': Wu, 'Wd': Wd}
    _L0_xattn_all = _L0_xattn_setup()
    _L0_xattn_in = {k: v for k, v in _L0_xattn_all.items() if k in ()}
    del _L0_xattn_all

    def _L0_ffn_setup():
        import jax, jax.numpy as jnp
        import numpy as np
        B, S, H = (2, 256, 512)
        E, K = (8, 2)
        F = 352
        FS = 1408
        NORM_TOPK = False

        def _swiglu(x, wg, wu, wd):
            return jax.nn.silu(x @ wg) * (x @ wu) @ wd
        key = jax.random.key(seed)
        ks = jax.random.split(key, 9)
        s = 0.02
        return {'hidden_states': jax.random.normal(ks[0], (B, S, H), dtype=jnp.float32), 'Wr': jax.random.normal(ks[1], (H, E), dtype=jnp.float32) * s, 'Wg': jax.random.normal(ks[2], (E, H, F), dtype=jnp.float32) * s, 'Wu': jax.random.normal(ks[3], (E, H, F), dtype=jnp.float32) * s, 'Wd': jax.random.normal(ks[4], (E, F, H), dtype=jnp.float32) * s, 'Sg': jax.random.normal(ks[5], (H, FS), dtype=jnp.float32) * s, 'Su': jax.random.normal(ks[6], (H, FS), dtype=jnp.float32) * s, 'Sd': jax.random.normal(ks[7], (FS, H), dtype=jnp.float32) * s, 'Wsg': jax.random.normal(ks[8], (H, 1), dtype=jnp.float32) * s}
    _L0_ffn_all = _L0_ffn_setup()
    _L0_ffn_in = {k: v for k, v in _L0_ffn_all.items() if k in ('Wr', 'Wg', 'Wu', 'Wd', 'Sg', 'Su', 'Sd', 'Wsg')}
    del _L0_ffn_all
    return {'x': x, 'itok_BxS_13_99985': itok_BxS_13_99985, 'ctx_2048': ctx_2048, 'L0_attn_w_attn': _L0_attn_in['w_attn'], 'L0_attn_b_attn': _L0_attn_in['b_attn'], 'L0_attn_w_proj': _L0_attn_in['w_proj'], 'L0_attn_b_proj': _L0_attn_in['b_proj'], 'L0_ffn_Wr': _L0_ffn_in['Wr'], 'L0_ffn_Wg': _L0_ffn_in['Wg'], 'L0_ffn_Wu': _L0_ffn_in['Wu'], 'L0_ffn_Wd': _L0_ffn_in['Wd'], 'L0_ffn_Sg': _L0_ffn_in['Sg'], 'L0_ffn_Su': _L0_ffn_in['Su'], 'L0_ffn_Sd': _L0_ffn_in['Sd'], 'L0_ffn_Wsg': _L0_ffn_in['Wsg']}

def reference(x, itok_BxS_13_99985, ctx_2048, L0_attn_w_attn, L0_attn_b_attn, L0_attn_w_proj, L0_attn_b_proj, L0_ffn_Wr, L0_ffn_Wg, L0_ffn_Wu, L0_ffn_Wd, L0_ffn_Sg, L0_ffn_Su, L0_ffn_Sd, L0_ffn_Wsg):
    import jax
    import jax.numpy as jnp

    def _L0_attn_ref(x, w_attn, b_attn, w_proj, b_proj):
        import jax, jax.numpy as jnp
        import numpy as np
        N_HEAD = 16
        B, T, C = x.shape
        hs = C // N_HEAD
        qkv = x @ w_attn + b_attn
        q, k, v = jnp.split(qkv, 3, axis=2)

        def _reshape(t):
            return t.reshape(B, T, N_HEAD, hs).transpose(0, 2, 1, 3)
        q, k, v = (_reshape(q), _reshape(k), _reshape(v))
        att = jnp.einsum('bhqd,bhkd->bhqk', q, k) * (1.0 / np.sqrt(hs))
        causal = jnp.tril(jnp.ones((T, T), dtype=bool))
        att = jnp.where(causal, att, -jnp.inf)
        att = jax.nn.softmax(att, axis=-1)
        y = jnp.einsum('bhqk,bhkd->bhqd', att, v)
        y = y.transpose(0, 2, 1, 3).reshape(B, T, C)
        return y @ w_proj + b_proj

    def _L0_xattn_ref(hidden_states, token_ids, Wg, Wu, Wd):
        import jax, jax.numpy as jnp
        import numpy as np
        B, S, D = (4, 1024, 512)
        E = 4
        F = 2048 // E
        VOCAB = 25000
        tokens_per_expert = VOCAB // E
        tid = jnp.clip(token_ids, 0, VOCAB - 1)
        expert_ids = jnp.minimum(tid // tokens_per_expert, E - 1)
        out = jnp.zeros_like(hidden_states)
        for e in range(E):
            g = jax.nn.silu(jnp.einsum('bsd,fd->bsf', hidden_states, Wg[e]))
            u = jnp.einsum('bsd,fd->bsf', hidden_states, Wu[e])
            y = jnp.einsum('bsf,df->bsd', g * u, Wd[e])
            out = jnp.where((expert_ids == e)[..., None], y, out)
        return out

    def _L0_ffn_ref(hidden_states, Wr, Wg, Wu, Wd, Sg, Su, Sd, Wsg):
        import jax, jax.numpy as jnp
        import numpy as np
        B, S, H = (2, 256, 512)
        E, K = (8, 2)
        F = 352
        FS = 1408
        NORM_TOPK = False

        def _swiglu(x, wg, wu, wd):
            return jax.nn.silu(x @ wg) * (x @ wu) @ wd
        b, s, h = hidden_states.shape
        x = hidden_states.reshape(-1, h)
        router_logits = x @ Wr
        probs = jax.nn.softmax(router_logits.astype(jnp.float32), axis=-1)
        routing_weights, selected = jax.lax.top_k(probs, K)
        if NORM_TOPK:
            routing_weights = routing_weights / routing_weights.sum(-1, keepdims=True)
        routing_weights = routing_weights.astype(x.dtype)
        C = jnp.einsum('tk,tke->te', routing_weights, jax.nn.one_hot(selected, E, dtype=x.dtype))
        expert_out = jax.vmap(lambda wg, wu, wd: _swiglu(x, wg, wu, wd))(Wg, Wu, Wd)
        moe_out = jnp.einsum('te,eth->th', C, expert_out)
        shared = _swiglu(x, Sg, Su, Sd)
        shared = jax.nn.sigmoid(x @ Wsg) * shared
        out = (moe_out + shared).reshape(b, s, h)
        return out
    x = _layernorm(x + _L0_attn_ref(x, L0_attn_w_attn, L0_attn_b_attn, L0_attn_w_proj, L0_attn_b_proj), axis=-1)
    x = _layernorm(x + _L0_xattn_ref(x, itok_BxS_13_99985, ctx_2048, ctx_2048, ctx_2048), axis=-1)
    x = _layernorm(x + _L0_ffn_ref(x, L0_ffn_Wr, L0_ffn_Wg, L0_ffn_Wu, L0_ffn_Wd, L0_ffn_Sg, L0_ffn_Su, L0_ffn_Sd, L0_ffn_Wsg), axis=-1)
    return x

_drawn_inputs = setup_inputs


def setup_inputs(seed=0):
    import zlib

    import numpy as np

    out = dict(_drawn_inputs(seed))
    spreads = {'L0_attn_b_attn': (0.0, 0.1), 'L0_attn_b_proj': (0.0, 0.1)}
    factors = {'L0_ffn_Wr': 5.586,
     'L0_ffn_Wg': 4.946,
     'L0_ffn_Wu': 4.847,
     'L0_ffn_Wd': 4.833,
     'L0_ffn_Wsg': 48.247,
     'L0_ffn_Sg': 4.48,
     'L0_ffn_Su': 4.395,
     'L0_ffn_Sd': 4.391}
    for name, (base, spread) in spreads.items():
        noise = np.random.default_rng([zlib.crc32(name.encode()), seed]).standard_normal(out[name].shape)
        drawn = base * np.exp(spread * noise) if base else spread * noise
        out[name] = jnp.asarray(drawn.astype(out[name].dtype))
    for name, factor in factors.items():
        out[name] = (out[name] * factor).astype(out[name].dtype)
    return out
```

```python
from contextlib import ExitStack

import numpy as np

import concourse.bass as bass
from concourse import mybir

F32 = mybir.dt.float32
F32R = mybir.dt.float32r
F16 = mybir.dt.float16
BF16 = mybir.dt.bfloat16
I32 = mybir.dt.int32
ALU = mybir.AluOpType
ACT = mybir.ActivationFunctionType
AX = mybir.AxisListType.X

P = 128
EPS = 1e-5
ONE = 1
BELOW_ALL = -1e30
P_SCALE = 4096.0


def split_high(eng, high, value):
    return eng.tensor_copy(high, value)


def attention_phase(nc, x, w_attn, b_attn, w_proj, b_proj, x1_dram):
    B, T, C = x.shape
    H, D = 16, 32
    KC = C // P
    QT = T // P
    G = H // 4
    SCALE = float(D) ** -0.5
    AUX = 3 * D
    VW = 3 * D + 1
    P_OFF = [0, 4 * P, 7 * P, 9 * P]
    P_COLS = 10 * P

    steps = [("XT", i) for i in range(QT)]
    steps += [("Q", 0), ("K", 0), ("Q", 1), ("K", 1)] + [("V", i) for i in range(QT)]
    steps += [("P1", 0, i) for i in range(4)] + [("M", 0)]
    for g in range(G):
        for i in range(4):
            steps.append(("P2", g, i))
            if g + 1 < G:
                steps.append(("P1", g + 1, i))
            if i < 2 and g + 2 < G:
                steps.append(("QK"[i], g + 2))
            if g or i:
                n = 4 * g + i - 1
                steps.append(("PV", n // 4, n % 4))
        if g + 1 < G:
            steps.append(("M", g + 1))
    steps.append(("PV", G - 1, 3))
    steps += [("Y", 0), ("Y", 1), ("PR", 0), ("Y", 2), ("PR", 1), ("Y", 3), ("PR", 2), ("PR", 3)]

    shared = [s for s in steps if s[0] in ("XT", "Q", "K", "V", "M", "Y", "PR")]
    NSH = len(shared)
    inside = [s[0] == "M" or (s[0] in "QK" and s[1] >= 2) for s in shared]
    bank_of, turn = [], 0
    for n in range(NSH):
        bank_of.append(0 if inside[n] else turn % 2)
        turn += 1
    last_on = {}
    before = []
    for n in range(NSH):
        before.append(last_on.get(bank_of[n]))
        last_on[bank_of[n]] = n
    NH = 4 * G
    NHIGH = sum(s[0] in ("XT", "Q", "K", "Y") for s in shared)

    with ExitStack() as ctx:
        def sb(name, shape, dt):
            return ctx.enter_context(nc.sbuf_tensor(f"attn_{name}", shape, dt))

        def sem(name):
            return ctx.enter_context(nc.semaphore(f"attn_{name}"))

        w_hi = sb("w_hi", [P, KC, 3 * C], F32R)
        w_lo = sb("w_lo", [P, KC, 3 * C], F32R)
        wp_hi = sb("wp_hi", [P, KC, C], F32R)
        wp_lo = sb("wp_lo", [P, KC, C], F32R)
        x_in = sb("x_in", [P, QT, C], F32)
        x_res = sb("x_res", [P, 2, C], F32)
        xT_hi = sb("xT_hi", [P, KC, T], F32R)
        xT_lo = sb("xT_lo", [P, KC, T], F32R)
        ch_hi = sb("ch_hi", [P, 2, T], F32R)
        ch_lo = sb("ch_lo", [P, 2, T], F32R)
        qS = [sb(f"qS{s}", [P, 4, T], F32R) for s in range(3)]
        kS = [sb(f"kS{s}", [P, 4, T], F32R) for s in range(3)]
        v_f = sb("v_f", [P, 2, C], F32)
        v_aug = sb("v_aug", [P, QT, H, VW], BF16)
        p_hi = sb("p_hi", [P, 2, P_COLS], F16)
        p_lo = sb("p_lo", [P, 2, P_COLS], F16)
        p_f = sb("p_f", [P, P_COLS], F32)
        y = sb("y", [P, QT, C], F32)
        yT_hi = [xT_hi[:, :, s * P:(s + 1) * P] for s in range(2)]
        yT_lo = [xT_lo[:, :, s * P:(s + 1) * P] for s in range(2)]
        z = sb("z", [P, QT, C], F32)
        bqk = sb("bqk", [P, 2 * G], F32)
        bv = sb("bv", [P, C], F32)
        bp = sb("bp", [P, C], F32)
        ident = sb("ident", [P, P], F32)
        ident_b = sb("ident_b", [P, P], BF16)
        mask_qk = sb("mask_qk", [P, P], BF16)
        mask_kq = sb("mask_kq", [P, P], BF16)
        rowmax = sb("rowmax", [P, 2, QT, 4], F32)
        rsum = sb("rsum", [P, 2, QT], F32)
        ysum = sb("ysum", [P, QT, D], F32)
        ln_scale = sb("ln_scale", [P, 1], F32)
        stats = sb("stats", [P, QT, 6], F32)
        mv = sb("mv", [P, QT, 2], F32)
        veps = sb("veps", [P, QT], F32)
        powm = sb("powm", [P, QT], F32)
        rstd = sb("rstd", [P, QT], F32)

        psS = ctx.enter_context(nc.psum_tensor("psS", [P, 3, 512], F32))
        psE = ctx.enter_context(nc.psum_tensor("psE", [P, 3, 512], F32))
        psO = ctx.enter_context(nc.psum_tensor("psO", [P, 512], F32))
        psT = ctx.enter_context(nc.psum_tensor("psT", [P, 512], F32))
        bank = [psT[:, :], psS[:, 0, :]]
        S_AT = [(0, 0), (2, 0), (0, P), (1, 0)]
        E_AT = [(0, 0), (1, 0), (2, 0), (2, 2 * P)]

        zero_ready = sem("zero_ready")
        consts_ready = sem("consts_ready")
        w_in = [sem("w_in0"), sem("w_in1")]
        w_hi_done = sem("w_hi_done")
        w_lo_done = sem("w_lo_done")
        bias_in = sem("bias_in")
        aux_ready = sem("aux_ready")
        x_ready = sem("x_ready")
        xres_in = [sem("xres_in0"), sem("xres_in1")]
        sh_full = sem("sh_full")
        sh_high = sem("sh_high")
        sh_free = sem("sh_free")
        stack_in = sem("stack_in")
        s_full = sem("s_full")
        max_done = sem("max_done")
        e_full = sem("e_full")
        exp_done = sem("exp_done")
        plow_done = sem("plow_done")
        o_full = sem("o_full")
        o_parts = sem("o_parts")
        y_done = sem("y_done")
        v_part1 = sem("v_part1")
        v_rest1 = sem("v_rest1")
        v_part2 = sem("v_part2")
        v_ready = sem("v_ready")
        xb_ready = sem("xb_ready")
        stats_done = sem("stats_done")
        mv_done = sem("mv_done")
        veps_done = sem("veps_done")
        rstd_done = sem("rstd_done")
        x1_done = sem("x1_done")
        x1_out = sem("x1_out")

        idx = {s: n for n, s in enumerate(shared)}
        block = ctx.enter_context(nc.Block())

        @block.sync
        def _(sp):
            for k in range(KC):
                if k >= 2:
                    sp.wait_ge(w_lo_done, k - 1)
                sp.dma_start((y if k % 2 else z)[:, 0:3, :].rearrange("p a n -> p (a n)"),
                             w_attn[k * P:(k + 1) * P, :]).then_inc(w_in[k % 2], 16)
                if k == 0:
                    sp.dma_start(x_in[:], x[0].rearrange("(t p) c -> p t c", p=P)).then_inc(x_ready, 16)
                    sp.dma_start(bqk[:], b_attn[0:2 * C].rearrange("(c p) -> p c", p=P),
                                 allow_slow_non_contiguous=True).then_inc(bias_in, 16)
                    sp.dma_start(bv[:], b_attn[2 * C:3 * C].partition_broadcast(P)).then_inc(bias_in, 16)
                    sp.dma_start(bp[:], b_proj.partition_broadcast(P)).then_inc(bias_in, 16)
            sp.wait_ge(w_lo_done, KC - 1)
            sp.dma_start(z[:], w_proj.rearrange("(k p) n -> p k n", p=P)).then_inc(w_in[0], 16)
            with sp.Fori(0, B) as b:
                for s in steps:
                    if s[0] in "QK":
                        qk, g = "QK".index(s[0]), s[1]
                        sp.wait_ge(sh_free, ONE + b * NSH + idx[s] + 1)
                        dst = (qS, kS)[qk][g % 3]
                        parts = (ch_hi, ch_hi, ch_lo) if qk == 0 else (ch_hi, ch_lo, ch_hi)
                        for r, part in enumerate(parts):
                            for i in range(4):
                                sp.dma_start(dst[r * D:(r + 1) * D, i, :].bitcast(F32),
                                             part[i * D:(i + 1) * D, qk, :].bitcast(F32)).then_inc(stack_in, 16)
                    if s == ("K", 3):
                        nxt = x[bass.ds(sp.snap((b + 1) % B), 1)].rearrange("a (t p) c -> p (a t) c", p=P)
                        sp.wait_ge(sh_full, ONE + b * NSH + idx[("XT", QT - 1)] + 1)
                        sp.dma_start(x_in[:], nxt).then_inc(x_ready, 16)
                    for i in {("K", 3): (0, 1), ("Y", 2): (2,), ("Y", 3): (3,)}.get(s, ()):
                        sp.wait_ge(stats_done, ONE + b * QT + max(i - 1, 0))
                        sp.dma_start(x_res[:, i % 2, :], x[bass.ds(b, 1), i * P:(i + 1) * P, :]
                                     .rearrange("a p c -> p (a c)")).then_inc(xres_in[i % 2], 16)
                for i in range(QT):
                    sp.wait_ge(x1_done, b * QT + i + 1)
                    sp.dma_start(x1_dram[bass.ds(b, 1), i * P:(i + 1) * P, :]
                                 .rearrange("a p c -> p (a c)"), z[:, i, :]).then_inc(x1_out, 16)
            sp.wait_ge(x_ready, 16 * (B + 1))
            sp.wait_ge(x1_out, ONE + 16 * QT * B)

        @block.gpsimd
        def _(pool):
            for s in (sh_free, sh_full, stack_in, max_done, exp_done, o_full, plow_done, y_done, v_ready, stats_done, x1_out):
                pool.sem_inc(s, ONE)
            pool.memset(ident[:], 0.0).then_inc(zero_ready, 1)
            pool.memset(mask_qk[:], 0.0).then_inc(zero_ready, 1)
            pool.memset(mask_kq[:], 0.0).then_inc(zero_ready, 1)
            pool.memset(p_f[:, 0:4], 0.0).then_inc(zero_ready, 1)
            pool.memset(ln_scale[:], float(np.log(P_SCALE))).then_inc(consts_ready, 1)
            pool.memset(powm[:], -0.5).then_inc(consts_ready, 1)
            pool.memset(v_aug[:, :, :, 3 * D:VW], 1.0).then_inc(consts_ready, 1)
            pool.wait_ge(zero_ready, 4)
            pool.affine_select(out=ident[:], in_=ident[:], compare_op=ALU.not_equal, fill=1.0, base=0,
                               pattern=[[-1, P]], channel_multiplier=1).then_inc(zero_ready, 1)
            pool.affine_select(out=mask_qk[:], in_=mask_qk[:], compare_op=ALU.is_ge, fill=BELOW_ALL, base=0,
                               pattern=[[-1, P]], channel_multiplier=1).then_inc(consts_ready, 1)
            pool.affine_select(out=mask_kq[:], in_=mask_kq[:], compare_op=ALU.is_ge, fill=BELOW_ALL, base=0,
                               pattern=[[1, P]], channel_multiplier=-1).then_inc(consts_ready, 1)
            pool.affine_select(out=p_f[:, 0:4], in_=p_f[:, 0:4], compare_op=ALU.not_equal, fill=1.0, base=-AUX,
                               pattern=[[-1, 4]], channel_multiplier=1).then_inc(zero_ready, 1)
            pool.wait_ge(zero_ready, 6)
            pool.tensor_copy(ident_b[:], ident[:]).then_inc(consts_ready, 1)
            with pool.Fori(0, B) as b:
                for i in range(QT):
                    va = v_aug[:, i, :, :]
                    vf = v_f[:, i % 2, :].rearrange("p (h d) -> p h d", h=H)
                    pool.wait_ge(v_part1, b * QT + i + 1)
                    pool.tensor_tensor(vf, vf, va[:, :, 0:D], ALU.subtract).then_inc(v_rest1, 1)
                    pool.wait_ge(v_part2, b * QT + i + 1)
                    pool.tensor_tensor(va[:, :, 2 * D:3 * D], vf, va[:, :, D:2 * D], ALU.subtract).then_inc(v_ready, 1)
                for i in range(QT):
                    pool.wait_ge(xres_in[i % 2], b * 32 + 16 * (i // 2 + 1))
                    if i == 0:
                        pool.wait_ge(bias_in, 48)
                    pool.tensor_tensor(x_res[:, i % 2, :], x_res[:, i % 2, :], bp[:], ALU.add).then_inc(xb_ready, 1)
                pool.wait_ge(veps_done, b * 2 + 2)
                pool.tensor_tensor(rstd[:], veps[:], powm[:], ALU.pow).then_inc(rstd_done, 1)

        @block.tensor
        def _(pe):
            pe.wait_ge(consts_ready, 6)
            pe.wait_ge(zero_ready, 6)
            with pe.Fori(0, B) as b:
                def take(s):
                    n = idx[s]
                    if before[n] is None:
                        pe.wait_ge(sh_free, ONE + b * NSH)
                    else:
                        pe.wait_ge(sh_free, ONE + b * NSH + before[n] + 1)
                    return bank[bank_of[n]]

                def products(out, lhs, rhs):
                    n = 0
                    for a, c in ((0, 0), (0, 1), (1, 0)):
                        for k in range(KC):
                            last = pe.matmul(out, lhs[a](k), rhs[c](k), start=(n == 0), stop=(n == 3 * KC - 1))
                            n += 1
                    return last

                for s in steps:
                    kind = s[0]
                    if kind == "XT":
                        i = s[1]
                        out = take(s)
                        if i == 0:
                            pe.wait_ge(x_ready, b * 16 + 16)
                        for k in range(KC):
                            last = pe.transpose(out[:, k * P:(k + 1) * P], x_in[:, i, k * P:(k + 1) * P], ident[:])
                        last.then_inc(sh_full, 1)
                    elif kind in ("Q", "K"):
                        c0 = ("QK".index(kind) * C) + s[1] * P
                        out = take(s)
                        if s == ("Q", 0):
                            pe.wait_ge(w_lo_done, KC + 1)
                            pe.wait_ge(sh_free, ONE + b * NSH + QT)
                        products(out, [lambda k: w_hi[:, k, c0:c0 + P], lambda k: w_lo[:, k, c0:c0 + P]],
                                 [lambda k: xT_hi[:, k, :], lambda k: xT_lo[:, k, :]]).then_inc(sh_full, 1)
                    elif kind == "V":
                        t0 = s[1] * P
                        products(take(s), [lambda k: xT_hi[:, k, t0:t0 + P], lambda k: xT_lo[:, k, t0:t0 + P]],
                                 [lambda k: w_hi[:, k, 2 * C:3 * C], lambda k: w_lo[:, k, 2 * C:3 * C]]).then_inc(sh_full, 1)
                    elif kind == "P1":
                        g, i = s[1:]
                        n = 4 * g + i
                        pe.wait_ge(stack_in, ONE + (b * G + g + 1) * 16 * 24)
                        pe.wait_ge(max_done, ONE + b * NH + n)
                        if n == 0:
                            pe.wait_ge(sh_free, ONE + b * NSH + idx[("V", QT - 1)] + 1)
                        q, k = qS[g % 3], kS[g % 3]
                        for t in (0, 2, 3, 1):
                            bk, c0 = S_AT[t]
                            width = (t + 1) * P
                            pe.matmul(psS[:, bk, c0:c0 + width], q[0:AUX, i, t * P:(t + 1) * P], k[0:AUX, i, 0:width],
                                      start=True, stop=True)
                            last = pe.matmul(psS[:, bk, c0 + width - P:c0 + width], ident_b[:], mask_qk[:],
                                             start=False, stop=True, skip_group_check=True)
                        last.then_inc(s_full, 1)
                    elif kind == "M":
                        g = s[1]
                        out = take(s)
                        pe.wait_ge(max_done, ONE + b * NH + 4 * g + 4)
                        for t in range(QT):
                            last = pe.transpose(out[0:4, t * P:(t + 1) * P], rowmax[:, g % 2, t, :], ident[:])
                        last.then_inc(sh_full, 1)
                    elif kind == "P2":
                        g, i = s[1:]
                        n = 4 * g + i
                        if i == 0:
                            pe.wait_ge(sh_free, ONE + b * NSH + idx[("M", g)] + 1)
                        pe.wait_ge(exp_done, ONE + b * NH + n)
                        q, k = qS[g % 3], kS[g % 3]
                        for j in range(QT):
                            bk, c0 = E_AT[j]
                            width = (QT - j) * P
                            pe.matmul(psE[:, bk, c0:c0 + width], k[0:AUX + 4, i, j * P:(j + 1) * P],
                                      q[0:AUX + 4, i, j * P:T], start=True, stop=True)
                            last = pe.matmul(psE[:, bk, c0:c0 + P], ident_b[:], mask_kq[:],
                                             start=False, stop=True, skip_group_check=True)
                        last.then_inc(e_full, 1)
                    elif kind == "PV":
                        g, i = s[1:]
                        n = 4 * g + i
                        if n == 0:
                            pe.wait_ge(v_ready, ONE + (b + 1) * QT)
                        pe.wait_ge(y_done, ONE + b * NH + n)
                        pe.wait_ge(plow_done, ONE + b * NH + n + 1)
                        for t in range(QT):
                            for j in range(t + 1):
                                c0 = P_OFF[j] + (t - j) * P
                                for m, part in enumerate((p_hi, p_lo)):
                                    last = pe.matmul(psO[:, t * VW:(t + 1) * VW], part[:, n % 2, c0:c0 + P],
                                                     v_aug[:, j, n, :], start=(j == 0 and m == 0),
                                                     stop=(j == t and m == 1))
                        last.then_inc(o_full, 1)
                    elif kind == "Y":
                        i = s[1]
                        out = take(s)
                        pe.wait_ge(y_done, ONE + (b + 1) * NH)
                        for k in range(KC):
                            last = pe.transpose(out[:, k * P:(k + 1) * P], y[:, i, k * P:(k + 1) * P], ident[:])
                        last.then_inc(sh_full, 1)
                    elif kind == "PR":
                        i = s[1]
                        out = take(s)
                        pe.wait_ge(sh_free, ONE + b * NSH + idx[("Y", i)] + 1)
                        products(out, [lambda k: yT_hi[i % 2][:, k, :], lambda k: yT_lo[i % 2][:, k, :]],
                                 [lambda k: wp_hi[:, k, :], lambda k: wp_lo[:, k, :]]).then_inc(sh_full, 1)

        @block.scalar
        def _(act):
            for k in range(KC):
                act.wait_ge(w_in[k % 2], 16 * (k // 2 + 1))
                act.copy(w_hi[:, k, :], (y if k % 2 else z)[:, 0:3, :].rearrange("p a n -> p (a n)")).then_inc(w_hi_done, 1)
            act.wait_ge(w_in[0], 16 * 3)
            act.copy(wp_hi[:], z[:]).then_inc(w_hi_done, 1)
            act.wait_ge(bias_in, 48)
            act.wait_ge(consts_ready, 6)
            with act.Fori(0, B) as b:
                for s in steps:
                    kind = s[0]
                    n = idx.get(s)
                    if kind == "XT":
                        i = s[1]
                        act.wait_ge(sh_full, ONE + b * NSH + n + 1)
                        act.copy(xT_hi[:, :, i * P:(i + 1) * P], bank[bank_of[n]].rearrange("p (k t) -> p k t", k=KC)).then_inc(sh_high, 1)
                    elif kind in ("Q", "K"):
                        qk = "QK".index(kind)
                        act.wait_ge(sh_full, ONE + b * NSH + n + 1)
                        act.wait_ge(stack_in, ONE + (b * G + s[1]) * 16 * 24)
                        act.activation(ch_hi[:, qk, :], bank[bank_of[n]], ACT.Identity,
                                       bias=bqk[:, qk * G + s[1]:qk * G + s[1] + 1]).then_inc(sh_high, 1)
                    elif kind == "V":
                        i = s[1]
                        va = v_aug[:, i, :, :]
                        vf = v_f[:, i % 2, :].rearrange("p (h d) -> p h d", h=H)
                        act.wait_ge(sh_free, ONE + b * NSH + n + 1)
                        act.copy(va[:, :, 0:D], vf).then_inc(v_part1, 1)
                        act.wait_ge(v_rest1, b * QT + i + 1)
                        act.copy(va[:, :, D:2 * D], vf).then_inc(v_part2, 1)
                    elif kind == "M":
                        act.wait_ge(sh_full, ONE + b * NSH + n + 1)
                        act.mul(qS[s[1] % 3][AUX:AUX + 4, :, :], bank[bank_of[n]][0:4, :].unsqueeze(1).broadcast_to([4, 4, T]),
                                -1.0).then_inc(sh_free, 1)
                    elif kind == "P2":
                        m = 4 * s[1] + s[2]
                        act.wait_ge(e_full, b * NH + m + 1)
                        act.wait_ge(o_full, ONE + b * NH + max(m - 1, 0))
                        act.activation(p_hi[:, m % 2, 0:4 * P], psE[:, 0, :], ACT.Exp, bias=ln_scale[:], scale=SCALE)
                        act.activation(p_hi[:, m % 2, 4 * P:P_COLS].rearrange("p (a n) -> p a n", a=2), psE[:, 1:3, 0:3 * P],
                                       ACT.Exp, bias=ln_scale[:], scale=SCALE)
                        act.wait_ge(plow_done, ONE + b * NH + m)
                        act.activation(p_f[:, 0:4 * P], psE[:, 0, :], ACT.Exp, bias=ln_scale[:], scale=SCALE)
                        act.activation(p_f[:, 4 * P:P_COLS].rearrange("p (a n) -> p a n", a=2), psE[:, 1:3, 0:3 * P],
                                       ACT.Exp, bias=ln_scale[:], scale=SCALE).then_inc(exp_done, 1)
                    elif kind == "Y":
                        act.wait_ge(sh_full, ONE + b * NSH + n + 1)
                        if s[1] >= 2:
                            act.wait_ge(sh_full, ONE + b * NSH + idx[("PR", s[1] - 2)] + 1)
                        act.copy(yT_hi[s[1] % 2], bank[bank_of[n]].rearrange("p (k t) -> p k t", k=KC)).then_inc(sh_high, 1)

        @block.vector
        def _(dve):
            for k in range(KC):
                dve.wait_ge(w_hi_done, k + 1)
                dve.tensor_tensor(w_lo[:, k, :], (y if k % 2 else z)[:, 0:3, :].rearrange("p a n -> p (a n)"),
                                  w_hi[:, k, :].bitcast(F32), ALU.subtract).then_inc(w_lo_done, 1)
            dve.wait_ge(w_hi_done, KC + 1)
            dve.tensor_tensor(wp_lo[:], z[:], wp_hi[:].bitcast(F32), ALU.subtract).then_inc(w_lo_done, 1)
            dve.wait_ge(zero_ready, 6)
            for s in range(3):
                dve.tensor_copy(kS[s][AUX:AUX + 4, :, :],
                                p_f[AUX:AUX + 4, 0:4].unsqueeze(2).broadcast_to([4, 4, T])).then_inc(aux_ready, 1)
            dve.wait_ge(bias_in, 48)
            with dve.Fori(0, B) as b:
                hi_n = 0
                for s in steps:
                    kind = s[0]
                    n = idx.get(s)
                    if kind in ("XT", "Q", "K", "Y"):
                        hi_n += 1
                        dve.wait_ge(sh_high, b * NHIGH + hi_n)
                    if kind == "XT":
                        i = s[1]
                        dst = (slice(None), slice(None), slice(i * P, (i + 1) * P))
                        dve.tensor_tensor(xT_lo[dst], bank[bank_of[n]].rearrange("p (k t) -> p k t", k=KC),
                                          xT_hi[dst].bitcast(F32), ALU.subtract).then_inc(sh_free, 1)
                    elif kind in ("Q", "K"):
                        qk = "QK".index(kind)
                        dve.scalar_tensor_tensor(ch_lo[:, qk, :], bank[bank_of[n]], bqk[:, qk * G + s[1]:qk * G + s[1] + 1],
                                                 ch_hi[:, qk, :].bitcast(F32), ALU.add, ALU.subtract).then_inc(sh_free, 1)
                    elif kind == "V":
                        i = s[1]
                        dve.wait_ge(sh_full, ONE + b * NSH + n + 1)
                        dve.wait_ge(v_ready, ONE + b * QT + max(i - 1, 0))
                        if i == 0:
                            dve.wait_ge(o_full, ONE + b * NH)
                        dve.tensor_tensor(v_f[:, i % 2, :], bank[bank_of[n]], bv[:], ALU.add).then_inc(sh_free, 1)
                    elif kind == "P1":
                        g, i = s[1:]
                        m = 4 * g + i
                        dve.wait_ge(s_full, b * NH + m + 1)
                        if i == 0:
                            dve.wait_ge(sh_full, ONE + b * NSH + (idx[("M", g - 2)] + 1 if g >= 2 else 0))
                        for t in range(QT):
                            bk, c0 = S_AT[t]
                            last = dve.tensor_reduce(rowmax[:, g % 2, t, i:i + 1], psS[:, bk, c0:c0 + (t + 1) * P], AX, ALU.max)
                        last.then_inc(max_done, 1)
                    elif kind == "P2":
                        m = 4 * s[1] + s[2]
                        dve.wait_ge(exp_done, ONE + b * NH + m + 1)
                        dve.tensor_tensor(p_lo[:, m % 2, :], p_f[:], p_hi[:, m % 2, :], ALU.subtract).then_inc(plow_done, 1)
                    elif kind == "PV":
                        m = 4 * s[1] + s[2]
                        dve.wait_ge(o_full, ONE + b * NH + m + 1)
                        if m == 0:
                            dve.wait_ge(sh_full, ONE + b * NSH)
                        o = psO[:, 0:QT * VW].rearrange("p (t c) -> p t c", t=QT)
                        dve.reciprocal(rsum[:, m % 2, :], o[:, :, 3 * D]).then_inc(o_parts, 1)
                        dve.tensor_reduce(ysum[:], o[:, :, 0:3 * D].rearrange("p t (s d) -> p t d s", s=3), AX, ALU.add).then_inc(o_parts, 1)
                        dve.wait_ge(o_parts, (b * NH + m) * 2 + 2)
                        dve.tensor_tensor(y[:, :, m * D:(m + 1) * D], ysum[:],
                                          rsum[:, m % 2, :].unsqueeze(2).broadcast_to([P, QT, D]), ALU.mult).then_inc(y_done, 1)
                    elif kind == "Y":
                        dve.tensor_tensor(yT_lo[s[1] % 2], bank[bank_of[n]].rearrange("p (k t) -> p k t", k=KC),
                                          yT_hi[s[1] % 2].bitcast(F32), ALU.subtract).then_inc(sh_free, 1)
                    elif kind == "PR":
                        i = s[1]
                        dve.wait_ge(sh_full, ONE + b * NSH + n + 1)
                        dve.wait_ge(xb_ready, b * QT + i + 1)
                        if i == 0:
                            dve.wait_ge(x1_out, ONE + b * 16 * QT)
                        dve.tensor_tensor(z[:, i, :], bank[bank_of[n]], x_res[:, i % 2, :], ALU.add).then_inc(sh_free, 1)
                        dve.wait_ge(sh_free, ONE + b * NSH + n + 1)
                        dve.bn_stats(stats[:, i, :], z[:, i, :]).then_inc(stats_done, 1)
                dve.wait_ge(stats_done, ONE + (b + 1) * QT)
                dve.memset(veps[:], EPS).then_inc(veps_done, 1)
                for i in range(QT):
                    dve.bn_aggr(mv[:, i, :], stats[:, i, :]).then_inc(mv_done, 1)
                dve.wait_ge(mv_done, (b + 1) * QT)
                dve.wait_ge(veps_done, b * 2 + 1)
                dve.tensor_tensor(veps[:], veps[:], mv[:, :, 1], ALU.add).then_inc(veps_done, 1)
                dve.wait_ge(rstd_done, b + 1)
                for i in range(QT):
                    dve.tensor_scalar(z[:, i, :], z[:, i, :], mv[:, i, 0:1], rstd[:, i:i + 1],
                                      ALU.subtract, ALU.mult).then_inc(x1_done, 1)


def expert_phase(nc, x_dram, out_dram, tokens=None, ctx_w=None, router=None, experts=None, shared=None):
    N, C = x_dram.shape
    NT = N // P
    KC = C // P
    BT = 4
    NB = NT // BT
    chosen = ctx_w is not None
    if chosen:
        E, F = ctx_w.shape[0], ctx_w.shape[1]
        SH = 0
    else:
        E, F = experts[0].shape[0], experts[0].shape[2]
        SH = shared[0].shape[1] // F
    FC = -(-F // P)
    rows = [min(P, F - f * P) for f in range(FC)]
    NE = E + SH
    PART = FC * C
    RW = E + 1

    tag = "chosen" if chosen else "routed"

    with ExitStack() as ctx:
        def sb(name, shape, dt):
            return ctx.enter_context(nc.sbuf_tensor(f"{tag}_{name}", shape, dt))

        def sem(name):
            return ctx.enter_context(nc.semaphore(f"{tag}_{name}"))

        xT_hi = sb("xT_hi", [P, KC, N], F32R)
        xT_lo = sb("xT_lo", [P, KC, N], F32R)
        acc = sb("acc", [P, NT, C], F32)
        NM = 1 if chosen else 3
        raw = sb("raw", [P, 2, PART if not chosen else KC * C], F32)
        wshape = [[P, KC, C]] if chosen else [[P, KC, F], [P, KC, F], [P, FC, C]]
        w_hi = [[sb(f"w_hi_{s}_{m}", wshape[m], F32R) for m in range(NM)] for s in range(2)]
        w_lo = [[sb(f"w_lo_{s}_{m}", wshape[m], F32R) for m in range(NM)] for s in range(2)]
        silu = sb("silu", [P, BT * P], F32)
        h_f = sb("h_f", [P, BT * P], F32)
        h_hi = sb("h_hi", [P, FC, BT * P], F32R)
        h_lo = sb("h_lo", [P, FC, BT * P], F32R)
        coef = sb("coef", [P, NE, NT], F32)
        ident = sb("ident", [P, P], F32)
        stats = sb("stats", [P, NT, 6], F32)
        mv = sb("mv", [P, NT, 2], F32)
        veps = sb("veps", [P, NT], F32)
        powm = sb("powm", [P, NT], F32)
        rstd = sb("rstd", [P, NT], F32)
        if chosen:
            tid = sb("tid", [P, NT], I32)
            above = sb("above", [P, E + 1, NT], F32)
        else:
            wr_raw = sb("wr_raw", [P, KC, RW], F32)
            wr_hi = sb("wr_hi", [P, KC, RW], F32R)
            wr_lo = sb("wr_lo", [P, KC, RW], F32R)
            lgT = sb("lgT", [RW, 512], F32)
            lg = sb("lg", [P, NT, RW], F32)
            ex = sb("ex", [P, NT, E], F32)
            pr = sb("pr", [P, NT, E], F32)
            row = sb("row", [P, NT], F32)
            before = sb("before", [P, E, E], F32)
            rank = sb("rank", [P, NT, E], F32)

        psG = ctx.enter_context(nc.psum_tensor(f"{tag}_psG", [P, 2, 512], F32))
        psU = ctx.enter_context(nc.psum_tensor(f"{tag}_psU", [P, 2, 512], F32))
        psY = ctx.enter_context(nc.psum_tensor(f"{tag}_psY", [P, 2, 512], F32))
        psT = ctx.enter_context(nc.psum_tensor(f"{tag}_psT2", [P, 2, 512], F32))

        x_in = [sem(f"x_in{i}") for i in range(4)]
        small_in = sem("small_in")
        zero_done = sem("zero_done")
        const_done = sem("const_done")
        raw_in = [sem("raw_in0"), sem("raw_in1")]
        t_full = sem("t_full")
        t_high = sem("t_high")
        t_free = sem("t_free")
        wr_done = sem("wr_done")
        coef_step = sem("coef_step")
        coef_done = sem("coef_done")
        wh_done = sem("wh_done")
        wl_done = sem("wl_done")
        up_full = sem("up_full")
        silu_done = sem("silu_done")
        hf_done = sem("hf_done")
        hh_done = sem("hh_done")
        hl_done = sem("hl_done")
        y_full = sem("y_full")
        y_added = sem("y_added")
        stats_done = sem("stats_done")
        mv_done = sem("mv_done")
        veps_done = sem("veps_done")
        rstd_done = sem("rstd_done")
        out_done = sem("out_done")
        stored = sem("stored")

        T0 = NT + (0 if chosen else NB + NT)
        TE = KC if chosen else 0
        TH0 = NT
        UPE, YPE = NB * FC, NT
        block = ctx.enter_context(nc.Block())

        def bank_of(n):
            return psT[:, n % 2, :]

        def loads(e, m, sh):
            if chosen:
                return ctx_w[bass.ds(e, 1)].rearrange("a (k p) f -> p (a k) f", p=P)
            if not sh:
                w = experts[m][bass.ds(e, 1)]
                if m < 2:
                    return w.rearrange("a (k p) f -> p (a k) f", p=P)
                return w.rearrange("a f c -> (a f) c")
            if m < 2:
                return shared[m][:, bass.ds(e * F, F)].rearrange("(k p) f -> p k f", p=P)
            return shared[2][bass.ds(e * F, F), :]

        def raw_view(i, m):
            if chosen:
                return raw[:, i % 2, 0:KC * C].rearrange("p (k f) -> p k f", k=KC)
            if m < 2:
                return raw[:, i % 2, 0:KC * F].rearrange("p (k f) -> p k f", k=KC)
            return raw[:, i % 2, 0:FC * C].rearrange("p (k f) -> p k f", k=FC)

        spans = [(E // 2, False, 0)] + ([(SH // 2, True, E // 2)] if SH else [])

        @block.sync
        def _(sp):
            for q in range(NB):
                sp.dma_start(acc[:, q * BT:(q + 1) * BT, :],
                             x_dram[q * BT * P:(q + 1) * BT * P, :].rearrange("(t p) c -> p t c", p=P)).then_inc(x_in[q], 16)
            if chosen:
                sp.dma_start(tid[:], tokens.rearrange("(t p) -> p t", p=P), allow_slow_non_contiguous=True).then_inc(small_in, 16)
            else:
                sp.dma_start(wr_raw[:, :, 0:E], router[0].rearrange("(k p) e -> p k e", p=P)).then_inc(small_in, 16)
                sp.dma_start(wr_raw[:, :, E:RW], router[1].rearrange("(k p) e -> p k e", p=P),
                             allow_slow_non_contiguous=True).then_inc(small_in, 16)
            for turns, sh, t0 in spans:
                with sp.Fori(0, turns) as t:
                    for s in range(2):
                        for m in range(NM):
                            i = NM * s + m
                            done = (t + t0) * 2 * NM + i
                            e = sp.snap(t * 2 + s)
                            if chosen:
                                sp.wait_ge(t_free, T0 + (t + t0) * 2 * TE + max(s - 1, 0) * TE)
                            else:
                                sp.wait_ge(wl_done, ONE + (t + t0) * 2 * NM + max(i - 1, 0))
                            src = loads(e, m, sh)
                            if m < 2:
                                sp.dma_start(raw_view(i, m), src).then_inc(raw_in[i % 2], 16)
                            else:
                                full = F // P
                                sp.dma_start(raw_view(i, m)[:, 0:full, :], src[0:full * P, :]
                                             .rearrange("(k p) c -> p k c", p=P)).then_inc(raw_in[i % 2], 16)
                                sp.dma_start(raw_view(i, m)[0:rows[-1], full, :], src[full * P:F, :]).then_inc(raw_in[i % 2], 16)
            for q in range(NT):
                sp.wait_ge(out_done, q + 1)
                sp.dma_start(out_dram[q * P:(q + 1) * P, :], acc[:, q, :]).then_inc(stored, 16)
            sp.wait_ge(stored, 16 * NT)

        def raw_count(t, i):
            if chosen:
                return 16 * (t + 1)
            upto = [j for j in range(i + 1) if j % 2 == i % 2]
            per = sum(2 if j % NM == 2 else 1 for j in range(2 * NM) if j % 2 == i % 2)
            return 16 * (t * per + sum(2 if j % NM == 2 else 1 for j in upto))

        @block.gpsimd
        def _(pool):
            for s in (hf_done, y_added, y_full, hh_done, hl_done, wl_done):
                pool.sem_inc(s, ONE)
            pool.memset(ident[:], 0.0).then_inc(zero_done, 1)
            pool.memset(powm[:], -0.5).then_inc(const_done, 1)
            pool.wait_ge(zero_done, 1)
            pool.affine_select(out=ident[:], in_=ident[:], compare_op=ALU.not_equal, fill=1.0, base=0,
                               pattern=[[-1, P]], channel_multiplier=1).then_inc(const_done, 1)
            if not chosen:
                pool.memset(before[:], 1.0).then_inc(zero_done, 1)
                pool.wait_ge(zero_done, 2)
                pool.affine_select(out=before[:], in_=before[:], compare_op=ALU.is_gt, fill=0.0, base=0,
                                   pattern=[[1, E], [-1, E]], channel_multiplier=0).then_inc(const_done, 1)
            pool.wait_ge(veps_done, 1)
            pool.tensor_tensor(rstd[:], veps[:], powm[:], ALU.pow).then_inc(rstd_done, 1)

        @block.tensor
        def _(pe):
            pe.wait_ge(const_done, 2)

            def three(out, lhs, rhs, ks):
                n = 0
                for a, c in ((0, 0), (0, 1), (1, 0)):
                    for k in range(ks):
                        last = pe.matmul(out, lhs[a](k), rhs[c](k), start=(n == 0), stop=(n == 3 * ks - 1))
                        n += 1
                return last

            for t in range(NT):
                if t % BT == 0:
                    pe.wait_ge(x_in[t // BT], 16)
                if t >= 2:
                    pe.wait_ge(t_free, t - 1)
                for k in range(KC):
                    last = pe.transpose(bank_of(t)[:, k * P:(k + 1) * P], acc[:, t, k * P:(k + 1) * P], ident[:])
                last.then_inc(t_full, 1)
            if not chosen:
                pe.wait_ge(wr_done, 2)
                pe.wait_ge(t_free, NT)
                for q in range(NB):
                    n = NT + q
                    three(psG[0:RW, 0, :], [lambda k: wr_hi[:, k, :], lambda k: wr_lo[:, k, :]],
                          [lambda k: xT_hi[:, k, q * 512:(q + 1) * 512], lambda k: xT_lo[:, k, q * 512:(q + 1) * 512]],
                          KC).then_inc(t_full, 1)
                    pe.wait_ge(t_free, NT + q * (BT + 1) + 1)
                    for i in range(BT):
                        last = pe.transpose(bank_of(0)[:, i * RW:(i + 1) * RW], lgT[:, i * P:(i + 1) * P], ident[0:RW, 0:RW])
                    last.then_inc(t_full, 1)
                    pe.wait_ge(t_free, NT + (q + 1) * (BT + 1))
            for turns, sh, t0 in spans:
                with pe.Fori(0, turns) as tt:
                    t = tt + t0
                    for s in range(2):
                        if chosen:
                            pe.wait_ge(raw_in[s], 16 * (t + 1))
                            for k in range(KC):
                                pe.wait_ge(t_free, T0 + t * 2 * TE + max(s * TE + k - 1, 0))
                                for c in range(KC):
                                    last = pe.transpose(bank_of(k)[:, c * P:(c + 1) * P],
                                                        raw_view(s, 0)[:, k, c * P:(c + 1) * P], ident[:])
                                last.then_inc(t_full, 1)
                            pe.wait_ge(t_free, T0 + t * 2 * TE + (s + 1) * TE)
                        else:
                            pe.wait_ge(wl_done, ONE + t * 2 * NM + (s + 1) * NM)
                        wg_hi, wg_lo = w_hi[s][0], w_lo[s][0]
                        wu_hi, wu_lo = w_hi[s][1 % NM], w_lo[s][1 % NM]
                        wd_hi, wd_lo = w_hi[s][-1], w_lo[s][-1]
                        for q in range(NB):
                            xs = [lambda k: xT_hi[:, k, q * 512:(q + 1) * 512], lambda k: xT_lo[:, k, q * 512:(q + 1) * 512]]
                            for f in range(FC):
                                n = (s * NB + q) * FC + f
                                f0, f1 = f * P, f * P + rows[f]
                                pe.wait_ge(hf_done, ONE + t * 2 * UPE + max(n - 1, 0))
                                last = three(psG[0:rows[f], n % 2, :], [lambda k: wg_hi[:, k, f0:f1], lambda k: wg_lo[:, k, f0:f1]], xs, KC)
                                if not chosen:
                                    last = three(psU[0:rows[f], n % 2, :], [lambda k: wu_hi[:, k, f0:f1], lambda k: wu_lo[:, k, f0:f1]], xs, KC)
                                last.then_inc(up_full, 1)
                            pe.wait_ge(hl_done, ONE + t * 2 * UPE + (s * NB + q + 1) * FC)
                            for i in range(BT):
                                n = (s * NB + q) * BT + i
                                pe.wait_ge(y_added, ONE + t * 2 * YPE + max(n - 1, 0))
                                three(psY[:, n % 2, :],
                                      [lambda k: h_hi[0:rows[k], k, i * P:(i + 1) * P], lambda k: h_lo[0:rows[k], k, i * P:(i + 1) * P]],
                                      [lambda k: wd_hi[0:rows[k], k, :], lambda k: wd_lo[0:rows[k], k, :]], FC).then_inc(y_full, 1)

        @block.scalar
        def _(act):
            for t in range(NT):
                act.wait_ge(t_full, t + 1)
                act.copy(xT_hi[:, :, t * P:(t + 1) * P], bank_of(t).rearrange("p (k n) -> p k n", k=KC)).then_inc(t_high, 1)
            if not chosen:
                act.wait_ge(small_in, 32)
                act.copy(wr_hi[:], wr_raw[:]).then_inc(wr_done, 1)
                act.wait_ge(coef_step, 2)
                act.activation(ex[:], ex[:], ACT.Exp).then_inc(coef_step, 1)
                act.activation(lg[:, :, E], lg[:, :, E], ACT.Exp, scale=-1.0).then_inc(coef_step, 1)
            for turns, sh, t0 in spans:
                with act.Fori(0, turns) as tt:
                    t = tt + t0
                    for s in range(2):
                        if chosen:
                            for k in range(KC):
                                act.wait_ge(t_full, T0 + t * 2 * TE + s * TE + k + 1)
                                act.wait_ge(y_full, ONE + t * 2 * YPE)
                                act.copy(w_hi[s][0][:, :, k * P:(k + 1) * P], bank_of(k).rearrange("p (c n) -> p c n", c=KC)).then_inc(wh_done, 1)
                        else:
                            act.wait_ge(y_full, ONE + t * 2 * YPE)
                            for m in range(NM):
                                i = NM * s + m
                                act.wait_ge(raw_in[i % 2], raw_count(t, i))
                                if m < 2:
                                    act.copy(w_hi[s][m][:], raw_view(i, m)).then_inc(wh_done, 1)
                                else:
                                    act.copy(w_hi[s][m][:, 0:FC - 1, :], raw_view(i, m)[:, 0:FC - 1, :])
                                    act.copy(w_hi[s][m][0:rows[-1], FC - 1, :], raw_view(i, m)[0:rows[-1], FC - 1, :]).then_inc(wh_done, 1)
                        for q in range(NB):
                            for f in range(FC):
                                n = (s * NB + q) * FC + f
                                r = rows[f]
                                act.wait_ge(up_full, t * 2 * UPE + n + 1)
                                act.wait_ge(hf_done, ONE + t * 2 * UPE + n)
                                act.activation(silu[0:r, :], psG[0:r, n % 2, :], ACT.Silu).then_inc(silu_done, 1)
                                act.wait_ge(hf_done, ONE + t * 2 * UPE + n + 1)
                                act.wait_ge(y_full, ONE + t * 2 * YPE + (s * NB + q) * BT)
                                act.copy(h_hi[0:r, f, :], h_f[0:r, :]).then_inc(hh_done, 1)

        @block.vector
        def _(dve):
            n_step = [0]
            for t in range(NT):
                dve.wait_ge(t_high, t + 1)
                dst = (slice(None), slice(None), slice(t * P, (t + 1) * P))
                dve.tensor_tensor(xT_lo[dst], bank_of(t).rearrange("p (k n) -> p k n", k=KC), xT_hi[dst].bitcast(F32),
                                  ALU.subtract).then_inc(t_free, 1)
            if chosen:
                dve.wait_ge(small_in, 16)
                dve.memset(above[:, 0, :], 1.0).then_inc(coef_step, 1)
                dve.memset(above[:, E, :], 0.0).then_inc(coef_step, 1)
                for e in range(1, E):
                    dve.tensor_scalar(above[:, e, :], tid[:], float(25000 // E * e), None, ALU.is_ge).then_inc(coef_step, 1)
                dve.wait_ge(coef_step, E + 1)
                dve.tensor_tensor(coef[:], above[:, 0:E, :], above[:, 1:E + 1, :], ALU.subtract).then_inc(coef_done, 1)
                dve.wait_ge(coef_done, 1)
            else:
                dve.wait_ge(wr_done, 1)
                dve.tensor_tensor(wr_lo[:], wr_raw[:], wr_hi[:].bitcast(F32), ALU.subtract).then_inc(wr_done, 1)
                for q in range(NB):
                    dve.wait_ge(t_full, NT + 2 * q + 1)
                    dve.tensor_copy(lgT[:], psG[0:RW, 0, :]).then_inc(t_free, 1)
                    dve.wait_ge(t_full, NT + 2 * q + 2)
                    dve.tensor_copy(lg[:, q * BT:(q + 1) * BT, :], bank_of(0)[:, 0:BT * RW].rearrange("p (t e) -> p t e", t=BT)).then_inc(t_free, BT)
                dve.wait_ge(t_free, NT + NB * (BT + 1))
                l = lg[:, :, 0:E]
                dve.tensor_reduce(row[:], l, AX, ALU.max).then_inc(coef_step, 1)
                dve.wait_ge(coef_step, 1)
                dve.tensor_tensor(ex[:], l, row[:].unsqueeze(2).broadcast_to([P, NT, E]), ALU.subtract).then_inc(coef_step, 1)
                dve.wait_ge(coef_step, 4)
                dve.tensor_reduce(row[:], ex[:], AX, ALU.add).then_inc(coef_step, 1)
                dve.tensor_scalar(lg[:, :, E], lg[:, :, E], 1.0, None, ALU.add).then_inc(coef_step, 1)
                dve.wait_ge(coef_step, 6)
                dve.reciprocal(row[:], row[:]).then_inc(coef_step, 1)
                dve.reciprocal(coef[:, E, :], lg[:, :, E]).then_inc(coef_step, 1)
                dve.wait_ge(coef_step, 8)
                dve.tensor_tensor(pr[:], ex[:], row[:].unsqueeze(2).broadcast_to([P, NT, E]), ALU.mult).then_inc(coef_step, 1)
                for s in range(1, SH):
                    dve.tensor_copy(coef[:, E + s, :], coef[:, E, :]).then_inc(coef_done, 1)
                dve.wait_ge(coef_step, 9)
                dve.wait_ge(const_done, 3)
                step = 9
                HT = NT // 2
                full = [P, HT, E, E]
                larger = h_f[:].rearrange("p (t e j) -> p t e j", t=HT, e=E)
                same = silu[:].rearrange("p (t e j) -> p t e j", t=HT, e=E)
                for hf in range(2):
                    half = pr[:, hf * HT:(hf + 1) * HT, :]
                    own, other = half.unsqueeze(3).broadcast_to(full), half.unsqueeze(2).broadcast_to(full)
                    dve.tensor_tensor(larger, other, own, ALU.is_gt).then_inc(coef_step, 1)
                    dve.tensor_tensor(same, other, own, ALU.is_equal).then_inc(coef_step, 1)
                    dve.wait_ge(coef_step, step + 2)
                    dve.tensor_tensor(same, same, before[:].unsqueeze(1).broadcast_to(full), ALU.mult).then_inc(coef_step, 1)
                    dve.wait_ge(coef_step, step + 3)
                    dve.tensor_tensor(larger, larger, same, ALU.add).then_inc(coef_step, 1)
                    dve.wait_ge(coef_step, step + 4)
                    dve.tensor_reduce(rank[:, hf * HT:(hf + 1) * HT, :], larger, AX, ALU.add).then_inc(coef_step, 1)
                    dve.wait_ge(coef_step, step + 5)
                    step += 5
                dve.wait_ge(coef_step, step)
                dve.scalar_tensor_tensor(coef[:, 0:E, :].rearrange("p e t -> p t e"), rank[:], 2.0, pr[:], ALU.is_lt, ALU.mult).then_inc(coef_done, 1)
                dve.wait_ge(coef_done, SH)
            for turns, sh, t0 in spans:
                with dve.Fori(0, turns) as tt:
                    t = tt + t0
                    for s in range(2):
                        if chosen:
                            for k in range(KC):
                                dve.wait_ge(wh_done, t * 2 * TE + s * TE + k + 1)
                                dve.tensor_tensor(w_lo[s][0][:, :, k * P:(k + 1) * P], bank_of(k).rearrange("p (c n) -> p c n", c=KC),
                                                  w_hi[s][0][:, :, k * P:(k + 1) * P].bitcast(F32), ALU.subtract).then_inc(t_free, 1)
                        else:
                            for m in range(NM):
                                i = NM * s + m
                                dve.wait_ge(wh_done, t * 2 * NM + i + 1)
                                if m < 2:
                                    dve.tensor_tensor(w_lo[s][m][:], raw_view(i, m), w_hi[s][m][:].bitcast(F32), ALU.subtract).then_inc(wl_done, 1)
                                else:
                                    dve.tensor_tensor(w_lo[s][m][:, 0:FC - 1, :], raw_view(i, m)[:, 0:FC - 1, :],
                                                      w_hi[s][m][:, 0:FC - 1, :].bitcast(F32), ALU.subtract)
                                    r = rows[-1]
                                    dve.tensor_tensor(w_lo[s][m][0:r, FC - 1, :], raw_view(i, m)[0:r, FC - 1, :],
                                                      w_hi[s][m][0:r, FC - 1, :].bitcast(F32), ALU.subtract).then_inc(wl_done, 1)
                        for q in range(NB):
                            for f in range(FC):
                                n = (s * NB + q) * FC + f
                                r = rows[f]
                                dve.wait_ge(silu_done, t * 2 * UPE + n + 1)
                                dve.wait_ge(hh_done, ONE + t * 2 * UPE + n)
                                dve.wait_ge(hl_done, ONE + t * 2 * UPE + n)
                                up = psG if chosen else psU
                                dve.tensor_tensor(h_f[0:r, :], up[0:r, n % 2, :], silu[0:r, :], ALU.mult).then_inc(hf_done, 1)
                                dve.wait_ge(hh_done, ONE + t * 2 * UPE + n + 1)
                                dve.tensor_tensor(h_lo[0:r, f, :], h_f[0:r, :], h_hi[0:r, f, :].bitcast(F32), ALU.subtract).then_inc(hl_done, 1)
                            for i in range(BT):
                                n = (s * NB + q) * BT + i
                                tok = q * BT + i
                                dve.wait_ge(y_full, ONE + t * 2 * YPE + n + 1)
                                e = t * 2 + s
                                dve.scalar_tensor_tensor(acc[:, tok, :], psY[:, n % 2, :], coef[:, bass.ds(e, 1), tok], acc[:, tok, :],
                                                         ALU.mult, ALU.add).then_inc(y_added, 1)
            dve.wait_ge(y_added, ONE + NE * NT)
            for q in range(NT):
                dve.bn_stats(stats[:, q, :], acc[:, q, :]).then_inc(stats_done, 1)
            dve.wait_ge(stats_done, NT)
            for q in range(NT):
                dve.bn_aggr(mv[:, q, :], stats[:, q, :]).then_inc(mv_done, 1)
            dve.wait_ge(mv_done, NT)
            dve.tensor_scalar(veps[:], mv[:, :, 1], EPS, None, ALU.add).then_inc(veps_done, 1)
            dve.wait_ge(rstd_done, 1)
            for q in range(NT):
                dve.tensor_scalar(acc[:, q, :], acc[:, q, :], mv[:, q, 0:1], rstd[:, q:q + 1], ALU.subtract, ALU.mult).then_inc(out_done, 1)


def decoder_kernel(nc, x, itok, ctx_w, w_attn, b_attn, w_proj, b_proj, wr, wg, wu, wd, sg, su, sd, wsg, out):
    x1 = nc.dram_tensor("x1", x.shape, F32, kind="Internal").ap()
    x2 = nc.dram_tensor("x2", x.shape, F32, kind="Internal").ap()
    attention_phase(nc, x, w_attn, b_attn, w_proj, b_proj, x1)
    expert_phase(nc, x1.rearrange("b s d -> (b s) d"), x2.rearrange("b s d -> (b s) d"),
                 tokens=itok.rearrange("b s -> (b s)"), ctx_w=ctx_w)
    expert_phase(nc, x2.rearrange("b s d -> (b s) d"), out.rearrange("b s d -> (b s) d"),
                 router=(wr, wsg), experts=(wg, wu, wd), shared=(sg, su, sd))


_INS = ["x", "itok_BxS_13_99985", "ctx_2048", "L0_attn_w_attn", "L0_attn_b_attn", "L0_attn_w_proj", "L0_attn_b_proj",
        "L0_ffn_Wr", "L0_ffn_Wg", "L0_ffn_Wu", "L0_ffn_Wd", "L0_ffn_Sg", "L0_ffn_Su", "L0_ffn_Sd", "L0_ffn_Wsg"]
_OUTS = [((4, 512, 512), "float32")]


def kernel(**inputs):
    import numpy as _np
    import concourse.bacc as _bacc
    from concourse import mybir as _mybir
    from concourse.bass_utils import run_bass_kernel_spmd as _run

    nc = _bacc.Bacc("TRN2", target_bir_lowering=False, num_devices=1)
    arrays, args = {}, []
    for name in _INS:
        a = _np.ascontiguousarray(inputs[name])
        arrays[f"in_{name}_dram"] = a
        args.append(nc.dram_tensor(f"in_{name}_dram", a.shape, _mybir.dt.from_np(a.dtype), kind="ExternalInput").ap())
    for i, (shape, dtype) in enumerate(_OUTS):
        dt = _mybir.dt.from_np(_np.dtype(dtype))
        args.append(nc.dram_tensor(f"out_{i}_dram", shape, dt, kind="ExternalOutput").ap())
    decoder_kernel(nc, *args)
    r = _run(nc, [arrays], core_ids=[0])
    return r.results[0]["out_0_dram"]
```

```python
from contextlib import ExitStack

import numpy as np

import concourse.bass as bass
from concourse import mybir

F32 = mybir.dt.float32
F32R = mybir.dt.float32r
F16 = mybir.dt.float16
BF16 = mybir.dt.bfloat16
I32 = mybir.dt.int32
U32 = mybir.dt.uint32
ALU = mybir.AluOpType
ACT = mybir.ActivationFunctionType
AX = mybir.AxisListType.X

P = 128
EPS = 1e-5
ONE = 1
BELOW_ALL = -1e30
P_SCALE = 4096.0


def split_high(eng, high, value):
    return eng.tensor_copy(high, value)


def attention_phase(nc, sems, x, w_attn, b_attn, w_proj, b_proj, x1_dram, cleared=()):
    B, T, C = x.shape
    H, D = 16, 32
    KC = C // P
    QT = T // P
    G = H // 4
    SCALE = float(D) ** -0.5
    AUX = 3 * D
    VW = 3 * D + 1
    P_OFF = [0, 4 * P, 7 * P, 9 * P]
    P_COLS = 10 * P

    steps = [("XT", i) for i in range(QT)]
    steps += [("Q", 0), ("K", 0), ("Q", 1), ("K", 1)] + [("V", i) for i in range(QT)]
    steps += [("P1", 0, i) for i in range(4)] + [("M", 0)]
    for g in range(G):
        for i in range(4):
            steps.append(("P2", g, i))
            if g + 1 < G:
                steps.append(("P1", g + 1, i))
            if i < 2 and g + 2 < G:
                steps.append(("QK"[i], g + 2))
            if g or i:
                n = 4 * g + i - 1
                steps.append(("PV", n // 4, n % 4))
        if g + 1 < G:
            steps.append(("M", g + 1))
    steps.append(("PV", G - 1, 3))
    steps += [("Y", 0), ("Y", 1), ("PR", 0), ("Y", 2), ("PR", 1), ("Y", 3), ("PR", 2), ("PR", 3)]

    shared = [s for s in steps if s[0] in ("XT", "Q", "K", "V", "M", "Y", "PR")]
    NSH = len(shared)
    inside = [s[0] == "M" or (s[0] in "QK" and s[1] >= 2) for s in shared]
    bank_of, turn = [], 0
    for n in range(NSH):
        bank_of.append(0 if inside[n] else turn % 2)
        turn += 1
    last_on = {}
    before = []
    for n in range(NSH):
        before.append(last_on.get(bank_of[n]))
        last_on[bank_of[n]] = n
    NH = 4 * G
    NHIGH = sum(s[0] in ("XT", "Q", "K", "Y") for s in shared)

    with ExitStack() as ctx:
        def sb(name, shape, dt):
            return ctx.enter_context(nc.sbuf_tensor(f"attn_{name}", shape, dt))

        def sem(name):
            return sems.enter_context(nc.semaphore(f"attn_{name}"))

        w_hi = sb("w_hi", [P, KC, 3 * C], F32R)
        w_lo = sb("w_lo", [P, KC, 3 * C], F32R)
        wp_hi = sb("wp_hi", [P, KC, C], F32R)
        wp_lo = sb("wp_lo", [P, KC, C], F32R)
        x_in = sb("x_in", [P, QT, C], F32)
        x_res = sb("x_res", [P, 2, C], F32)
        xT_hi = sb("xT_hi", [P, KC, T], F32R)
        xT_lo = sb("xT_lo", [P, KC, T], F32R)
        ch_hi = sb("ch_hi", [P, 2, T], F32R)
        ch_lo = sb("ch_lo", [P, 2, T], F32R)
        qS = [sb(f"qS{s}", [P, 4, T], F32R) for s in range(3)]
        kS = [sb(f"kS{s}", [P, 4, T], F32R) for s in range(3)]
        v_f = sb("v_f", [P, 2, C], F32)
        v_aug = sb("v_aug", [P, QT, H, VW], BF16)
        p_hi = sb("p_hi", [P, 2, P_COLS], F16)
        p_lo = sb("p_lo", [P, 2, P_COLS], F16)
        p_f = sb("p_f", [P, P_COLS], F32)
        y = sb("y", [P, QT, C], F32)
        yT_hi = [xT_hi[:, :, s * P:(s + 1) * P] for s in range(2)]
        yT_lo = [xT_lo[:, :, s * P:(s + 1) * P] for s in range(2)]
        z = sb("z", [P, QT, C], F32)
        bqk = sb("bqk", [P, 2 * G], F32)
        bv = sb("bv", [P, C], F32)
        bp = sb("bp", [P, C], F32)
        ident = sb("ident", [P, P], F32)
        ident_b = sb("ident_b", [P, P], BF16)
        mask_qk = sb("mask_qk", [P, P], BF16)
        mask_kq = sb("mask_kq", [P, P], BF16)
        rowmax = sb("rowmax", [P, 2, QT, 4], F32)
        rsum = sb("rsum", [P, 2, QT], F32)
        ysum = sb("ysum", [P, QT, D], F32)
        ln_scale = sb("ln_scale", [P, 1], F32)
        stats = sb("stats", [P, QT, 6], F32)
        mv = sb("mv", [P, QT, 2], F32)
        veps = sb("veps", [P, QT], F32)
        powm = sb("powm", [P, QT], F32)
        zero = sb("zero", [P, C], F32)
        rstd = sb("rstd", [P, QT], F32)

        psS = ctx.enter_context(nc.psum_tensor("psS", [P, 3, 512], F32))
        psE = ctx.enter_context(nc.psum_tensor("psE", [P, 3, 512], F32))
        psO = ctx.enter_context(nc.psum_tensor("psO", [P, 512], F32))
        psT = ctx.enter_context(nc.psum_tensor("psT", [P, 512], F32))
        bank = [psT[:, :], psS[:, 0, :]]
        S_AT = [(0, 0), (2, 0), (0, P), (1, 0)]
        E_AT = [(0, 0), (1, 0), (2, 0), (2, 2 * P)]

        zero_ready = sem("zero_ready")
        nothing = sem("nothing")
        clear_done = sem("clear_done")
        consts_ready = sem("consts_ready")
        w_in = [sem("w_in0"), sem("w_in1")]
        w_hi_done = sem("w_hi_done")
        w_lo_done = sem("w_lo_done")
        bias_in = sem("bias_in")
        x_ready = sem("x_ready")
        xres_in = [sem("xres_in0"), sem("xres_in1")]
        sh_full = sem("sh_full")
        sh_high = sem("sh_high")
        sh_free = sem("sh_free")
        stack_in = sem("stack_in")
        s_full = sem("s_full")
        max_done = sem("max_done")
        e_full = sem("e_full")
        exp_done = sem("exp_done")
        plow_done = sem("plow_done")
        o_full = sem("o_full")
        o_parts = sem("o_parts")
        y_done = sem("y_done")
        v_part1 = sem("v_part1")
        v_rest1 = sem("v_rest1")
        v_part2 = sem("v_part2")
        v_ready = sem("v_ready")
        xb_ready = sem("xb_ready")
        stats_done = sem("stats_done")
        mv_done = sem("mv_done")
        veps_done = sem("veps_done")
        rstd_done = sem("rstd_done")
        x1_done = sem("x1_done")
        x1_out = sem("x1_out")

        idx = {s: n for n, s in enumerate(shared)}
        block = ctx.enter_context(nc.Block())

        @block.sync
        def _(sp):
            for k in range(KC):
                if k >= 2:
                    sp.wait_ge(w_lo_done, k - 1)
                sp.dma_start((y if k % 2 else z)[:, 0:3, :].rearrange("p a n -> p (a n)"),
                             w_attn[k * P:(k + 1) * P, :]).then_inc(w_in[k % 2], 16)
                if k == 0:
                    sp.dma_start(x_in[:], x[0].rearrange("(t p) c -> p t c", p=P)).then_inc(x_ready, 16)
                    sp.dma_start(bqk[:], b_attn[0:2 * C].rearrange("(c p) -> p c", p=P),
                                 allow_slow_non_contiguous=True).then_inc(bias_in, 16)
                    sp.dma_start(bv[:], b_attn[2 * C:3 * C].partition_broadcast(P)).then_inc(bias_in, 16)
                    sp.dma_start(bp[:], b_proj.partition_broadcast(P)).then_inc(bias_in, 16)
            sp.wait_ge(nothing, 1)
            for rows in cleared:
                n = rows.shape[0] // P
                sp.dma_start(rows.rearrange("(n p) c -> p n c", p=P), zero[:].unsqueeze(1).broadcast_to([P, n, C])).then_inc(clear_done, 16)
            sp.wait_ge(w_lo_done, KC - 1)
            sp.dma_start(z[:], w_proj.rearrange("(k p) n -> p k n", p=P)).then_inc(w_in[0], 16)
            with sp.Fori(0, B) as b:
                for s in steps:
                    if s[0] in "QK":
                        qk, g = "QK".index(s[0]), s[1]
                        sp.wait_ge(sh_free, ONE + b * NSH + idx[s] + 1)
                        dst = (qS, kS)[qk][g % 3]
                        parts = (ch_hi, ch_hi, ch_lo) if qk == 0 else (ch_hi, ch_lo, ch_hi)
                        for r, part in enumerate(parts):
                            for i in range(4):
                                sp.dma_start(dst[r * D:(r + 1) * D, i, :].bitcast(F32),
                                             part[i * D:(i + 1) * D, qk, :].bitcast(F32)).then_inc(stack_in, 16)
                    if s == ("K", 3):
                        nxt = x[bass.ds(sp.snap((b + 1) % B), 1)].rearrange("a (t p) c -> p (a t) c", p=P)
                        sp.wait_ge(sh_full, ONE + b * NSH + idx[("XT", QT - 1)] + 1)
                        sp.dma_start(x_in[:], nxt).then_inc(x_ready, 16)
                    for i in {("K", 3): (0, 1), ("Y", 2): (2,), ("Y", 3): (3,)}.get(s, ()):
                        sp.wait_ge(stats_done, ONE + b * QT + max(i - 1, 0))
                        sp.dma_start(x_res[:, i % 2, :], x[bass.ds(b, 1), i * P:(i + 1) * P, :]
                                     .rearrange("a p c -> p (a c)")).then_inc(xres_in[i % 2], 16)
                for i in range(QT):
                    sp.wait_ge(x1_done, b * QT + i + 1)
                    sp.dma_start(x1_dram[bass.ds(b, 1), i * P:(i + 1) * P, :]
                                 .rearrange("a p c -> p (a c)"), z[:, i, :]).then_inc(x1_out, 16)
            sp.wait_ge(x_ready, 16 * (B + 1))
            if cleared:
                sp.wait_ge(clear_done, 16 * len(cleared))
            sp.wait_ge(x1_out, ONE + 16 * QT * B)

        @block.gpsimd
        def _(pool):
            for s in (sh_free, sh_full, stack_in, max_done, exp_done, o_full, plow_done, y_done, v_ready, stats_done, x1_out):
                pool.sem_inc(s, ONE)
            pool.memset(zero[:], 0.0).then_inc(nothing, 1)
            pool.memset(ident[:], 0.0).then_inc(zero_ready, 1)
            pool.memset(mask_qk[:], 0.0).then_inc(zero_ready, 1)
            pool.memset(mask_kq[:], 0.0).then_inc(zero_ready, 1)
            pool.memset(p_f[:, 0:4], 0.0).then_inc(zero_ready, 1)
            pool.memset(ln_scale[:], float(np.log(P_SCALE))).then_inc(consts_ready, 1)
            pool.memset(powm[:], -0.5).then_inc(consts_ready, 1)
            pool.memset(v_aug[:, :, :, 3 * D:VW], 1.0).then_inc(consts_ready, 1)
            pool.wait_ge(zero_ready, 4)
            pool.affine_select(out=ident[:], in_=ident[:], compare_op=ALU.not_equal, fill=1.0, base=0,
                               pattern=[[-1, P]], channel_multiplier=1).then_inc(zero_ready, 1)
            pool.affine_select(out=mask_qk[:], in_=mask_qk[:], compare_op=ALU.is_ge, fill=BELOW_ALL, base=0,
                               pattern=[[-1, P]], channel_multiplier=1).then_inc(consts_ready, 1)
            pool.affine_select(out=mask_kq[:], in_=mask_kq[:], compare_op=ALU.is_ge, fill=BELOW_ALL, base=0,
                               pattern=[[1, P]], channel_multiplier=-1).then_inc(consts_ready, 1)
            pool.affine_select(out=p_f[:, 0:4], in_=p_f[:, 0:4], compare_op=ALU.not_equal, fill=1.0, base=-AUX,
                               pattern=[[-1, 4]], channel_multiplier=1).then_inc(zero_ready, 1)
            pool.wait_ge(zero_ready, 6)
            pool.tensor_copy(ident_b[:], ident[:]).then_inc(consts_ready, 1)
            with pool.Fori(0, B) as b:
                for i in range(QT):
                    va = v_aug[:, i, :, :]
                    vf = v_f[:, i % 2, :].rearrange("p (h d) -> p h d", h=H)
                    pool.wait_ge(v_part1, b * QT + i + 1)
                    pool.tensor_tensor(vf, vf, va[:, :, 0:D], ALU.subtract).then_inc(v_rest1, 1)
                    pool.wait_ge(v_part2, b * QT + i + 1)
                    pool.tensor_tensor(va[:, :, 2 * D:3 * D], vf, va[:, :, D:2 * D], ALU.subtract).then_inc(v_ready, 1)
                for i in range(QT):
                    pool.wait_ge(xres_in[i % 2], b * 32 + 16 * (i // 2 + 1))
                    if i == 0:
                        pool.wait_ge(bias_in, 48)
                    pool.tensor_tensor(x_res[:, i % 2, :], x_res[:, i % 2, :], bp[:], ALU.add).then_inc(xb_ready, 1)
                pool.wait_ge(veps_done, b * 2 + 2)
                pool.tensor_tensor(rstd[:], veps[:], powm[:], ALU.pow).then_inc(rstd_done, 1)

        @block.tensor
        def _(pe):
            pe.wait_ge(consts_ready, 6)
            pe.wait_ge(zero_ready, 6)
            with pe.Fori(0, B) as b:
                def take(s):
                    n = idx[s]
                    if before[n] is None:
                        pe.wait_ge(sh_free, ONE + b * NSH)
                    else:
                        pe.wait_ge(sh_free, ONE + b * NSH + before[n] + 1)
                    return bank[bank_of[n]]

                def products(out, lhs, rhs):
                    n = 0
                    for a, c in ((0, 0), (0, 1), (1, 0)):
                        for k in range(KC):
                            last = pe.matmul(out, lhs[a](k), rhs[c](k), start=(n == 0), stop=(n == 3 * KC - 1))
                            n += 1
                    return last

                for s in steps:
                    kind = s[0]
                    if kind == "XT":
                        i = s[1]
                        out = take(s)
                        if i == 0:
                            pe.wait_ge(x_ready, b * 16 + 16)
                        for k in range(KC):
                            last = pe.transpose(out[:, k * P:(k + 1) * P], x_in[:, i, k * P:(k + 1) * P], ident[:])
                        last.then_inc(sh_full, 1)
                    elif kind in ("Q", "K"):
                        c0 = ("QK".index(kind) * C) + s[1] * P
                        out = take(s)
                        if s == ("Q", 0):
                            pe.wait_ge(w_lo_done, KC + 1)
                            pe.wait_ge(sh_free, ONE + b * NSH + QT)
                        products(out, [lambda k: w_hi[:, k, c0:c0 + P], lambda k: w_lo[:, k, c0:c0 + P]],
                                 [lambda k: xT_hi[:, k, :], lambda k: xT_lo[:, k, :]]).then_inc(sh_full, 1)
                    elif kind == "V":
                        t0 = s[1] * P
                        products(take(s), [lambda k: xT_hi[:, k, t0:t0 + P], lambda k: xT_lo[:, k, t0:t0 + P]],
                                 [lambda k: w_hi[:, k, 2 * C:3 * C], lambda k: w_lo[:, k, 2 * C:3 * C]]).then_inc(sh_full, 1)
                    elif kind == "P1":
                        g, i = s[1:]
                        n = 4 * g + i
                        pe.wait_ge(stack_in, ONE + (b * G + g + 1) * 16 * 24)
                        pe.wait_ge(max_done, ONE + b * NH + n)
                        if n == 0:
                            pe.wait_ge(sh_free, ONE + b * NSH + idx[("V", QT - 1)] + 1)
                        q, k = qS[g % 3], kS[g % 3]
                        for t in (0, 2, 3, 1):
                            bk, c0 = S_AT[t]
                            width = (t + 1) * P
                            pe.matmul(psS[:, bk, c0:c0 + width], q[0:AUX, i, t * P:(t + 1) * P], k[0:AUX, i, 0:width],
                                      start=True, stop=True)
                            last = pe.matmul(psS[:, bk, c0 + width - P:c0 + width], ident_b[:], mask_qk[:],
                                             start=False, stop=True, skip_group_check=True)
                        last.then_inc(s_full, 1)
                    elif kind == "M":
                        g = s[1]
                        out = take(s)
                        pe.wait_ge(max_done, ONE + b * NH + 4 * g + 4)
                        for t in range(QT):
                            last = pe.transpose(out[0:4, t * P:(t + 1) * P], rowmax[:, g % 2, t, :], ident[:])
                        last.then_inc(sh_full, 1)
                    elif kind == "P2":
                        g, i = s[1:]
                        n = 4 * g + i
                        if i == 0:
                            pe.wait_ge(sh_free, ONE + b * NSH + idx[("M", g)] + 1)
                        pe.wait_ge(exp_done, ONE + b * NH + n)
                        q, k = qS[g % 3], kS[g % 3]
                        for j in range(QT):
                            bk, c0 = E_AT[j]
                            width = (QT - j) * P
                            pe.matmul(psE[:, bk, c0:c0 + width], k[0:AUX + 4, i, j * P:(j + 1) * P],
                                      q[0:AUX + 4, i, j * P:T], start=True, stop=True)
                            last = pe.matmul(psE[:, bk, c0:c0 + P], ident_b[:], mask_kq[:],
                                             start=False, stop=True, skip_group_check=True)
                        last.then_inc(e_full, 1)
                    elif kind == "PV":
                        g, i = s[1:]
                        n = 4 * g + i
                        if n == 0:
                            pe.wait_ge(v_ready, ONE + (b + 1) * QT)
                        pe.wait_ge(y_done, ONE + b * NH + n)
                        pe.wait_ge(plow_done, ONE + b * NH + n + 1)
                        for t in range(QT):
                            for j in range(t + 1):
                                c0 = P_OFF[j] + (t - j) * P
                                for m, part in enumerate((p_hi, p_lo)):
                                    last = pe.matmul(psO[:, t * VW:(t + 1) * VW], part[:, n % 2, c0:c0 + P],
                                                     v_aug[:, j, n, :], start=(j == 0 and m == 0),
                                                     stop=(j == t and m == 1))
                        last.then_inc(o_full, 1)
                    elif kind == "Y":
                        i = s[1]
                        out = take(s)
                        pe.wait_ge(y_done, ONE + (b + 1) * NH)
                        for k in range(KC):
                            last = pe.transpose(out[:, k * P:(k + 1) * P], y[:, i, k * P:(k + 1) * P], ident[:])
                        last.then_inc(sh_full, 1)
                    elif kind == "PR":
                        i = s[1]
                        out = take(s)
                        pe.wait_ge(sh_free, ONE + b * NSH + idx[("Y", i)] + 1)
                        products(out, [lambda k: yT_hi[i % 2][:, k, :], lambda k: yT_lo[i % 2][:, k, :]],
                                 [lambda k: wp_hi[:, k, :], lambda k: wp_lo[:, k, :]]).then_inc(sh_full, 1)

        @block.scalar
        def _(act):
            for k in range(KC):
                act.wait_ge(w_in[k % 2], 16 * (k // 2 + 1))
                act.copy(w_hi[:, k, :], (y if k % 2 else z)[:, 0:3, :].rearrange("p a n -> p (a n)")).then_inc(w_hi_done, 1)
            act.wait_ge(w_in[0], 16 * 3)
            act.copy(wp_hi[:], z[:]).then_inc(w_hi_done, 1)
            act.wait_ge(bias_in, 48)
            act.wait_ge(consts_ready, 6)
            with act.Fori(0, B) as b:
                for s in steps:
                    kind = s[0]
                    n = idx.get(s)
                    if kind == "XT":
                        i = s[1]
                        act.wait_ge(sh_full, ONE + b * NSH + n + 1)
                        act.copy(xT_hi[:, :, i * P:(i + 1) * P], bank[bank_of[n]].rearrange("p (k t) -> p k t", k=KC)).then_inc(sh_high, 1)
                    elif kind in ("Q", "K"):
                        qk = "QK".index(kind)
                        act.wait_ge(sh_full, ONE + b * NSH + n + 1)
                        act.wait_ge(stack_in, ONE + (b * G + s[1]) * 16 * 24)
                        act.activation(ch_hi[:, qk, :], bank[bank_of[n]], ACT.Identity,
                                       bias=bqk[:, qk * G + s[1]:qk * G + s[1] + 1]).then_inc(sh_high, 1)
                    elif kind == "V":
                        i = s[1]
                        va = v_aug[:, i, :, :]
                        vf = v_f[:, i % 2, :].rearrange("p (h d) -> p h d", h=H)
                        act.wait_ge(sh_free, ONE + b * NSH + n + 1)
                        act.copy(va[:, :, 0:D], vf).then_inc(v_part1, 1)
                        act.wait_ge(v_rest1, b * QT + i + 1)
                        act.copy(va[:, :, D:2 * D], vf).then_inc(v_part2, 1)
                    elif kind == "M":
                        act.wait_ge(sh_full, ONE + b * NSH + n + 1)
                        act.mul(qS[s[1] % 3][AUX:AUX + 4, :, :], bank[bank_of[n]][0:4, :].unsqueeze(1).broadcast_to([4, 4, T]),
                                -1.0).then_inc(sh_free, 1)
                    elif kind == "P2":
                        m = 4 * s[1] + s[2]
                        act.wait_ge(e_full, b * NH + m + 1)
                        act.wait_ge(o_full, ONE + b * NH + max(m - 1, 0))
                        act.activation(p_hi[:, m % 2, 0:4 * P], psE[:, 0, :], ACT.Exp, bias=ln_scale[:], scale=SCALE)
                        act.activation(p_hi[:, m % 2, 4 * P:P_COLS].rearrange("p (a n) -> p a n", a=2), psE[:, 1:3, 0:3 * P],
                                       ACT.Exp, bias=ln_scale[:], scale=SCALE)
                        act.wait_ge(plow_done, ONE + b * NH + m)
                        act.activation(p_f[:, 0:4 * P], psE[:, 0, :], ACT.Exp, bias=ln_scale[:], scale=SCALE)
                        act.activation(p_f[:, 4 * P:P_COLS].rearrange("p (a n) -> p a n", a=2), psE[:, 1:3, 0:3 * P],
                                       ACT.Exp, bias=ln_scale[:], scale=SCALE).then_inc(exp_done, 1)
                    elif kind == "Y":
                        act.wait_ge(sh_full, ONE + b * NSH + n + 1)
                        if s[1] >= 2:
                            act.wait_ge(sh_full, ONE + b * NSH + idx[("PR", s[1] - 2)] + 1)
                        act.copy(yT_hi[s[1] % 2], bank[bank_of[n]].rearrange("p (k t) -> p k t", k=KC)).then_inc(sh_high, 1)

        @block.vector
        def _(dve):
            for k in range(KC):
                dve.wait_ge(w_hi_done, k + 1)
                dve.tensor_tensor(w_lo[:, k, :], (y if k % 2 else z)[:, 0:3, :].rearrange("p a n -> p (a n)"),
                                  w_hi[:, k, :].bitcast(F32), ALU.subtract).then_inc(w_lo_done, 1)
            dve.wait_ge(w_hi_done, KC + 1)
            dve.tensor_tensor(wp_lo[:], z[:], wp_hi[:].bitcast(F32), ALU.subtract).then_inc(w_lo_done, 1)
            dve.wait_ge(zero_ready, 6)
            for s in range(3):
                dve.tensor_copy(kS[s][AUX:AUX + 4, :, :],
                                p_f[AUX:AUX + 4, 0:4].unsqueeze(2).broadcast_to([4, 4, T]))
            dve.wait_ge(bias_in, 48)
            with dve.Fori(0, B) as b:
                hi_n = 0
                for s in steps:
                    kind = s[0]
                    n = idx.get(s)
                    if kind in ("XT", "Q", "K", "Y"):
                        hi_n += 1
                        dve.wait_ge(sh_high, b * NHIGH + hi_n)
                    if kind == "XT":
                        i = s[1]
                        dst = (slice(None), slice(None), slice(i * P, (i + 1) * P))
                        dve.tensor_tensor(xT_lo[dst], bank[bank_of[n]].rearrange("p (k t) -> p k t", k=KC),
                                          xT_hi[dst].bitcast(F32), ALU.subtract).then_inc(sh_free, 1)
                    elif kind in ("Q", "K"):
                        qk = "QK".index(kind)
                        dve.scalar_tensor_tensor(ch_lo[:, qk, :], bank[bank_of[n]], bqk[:, qk * G + s[1]:qk * G + s[1] + 1],
                                                 ch_hi[:, qk, :].bitcast(F32), ALU.add, ALU.subtract).then_inc(sh_free, 1)
                    elif kind == "V":
                        i = s[1]
                        dve.wait_ge(sh_full, ONE + b * NSH + n + 1)
                        dve.wait_ge(v_ready, ONE + b * QT + max(i - 1, 0))
                        if i == 0:
                            dve.wait_ge(o_full, ONE + b * NH)
                        dve.tensor_tensor(v_f[:, i % 2, :], bank[bank_of[n]], bv[:], ALU.add).then_inc(sh_free, 1)
                    elif kind == "P1":
                        g, i = s[1:]
                        m = 4 * g + i
                        dve.wait_ge(s_full, b * NH + m + 1)
                        if i == 0:
                            dve.wait_ge(sh_full, ONE + b * NSH + (idx[("M", g - 2)] + 1 if g >= 2 else 0))
                        for t in range(QT):
                            bk, c0 = S_AT[t]
                            last = dve.tensor_reduce(rowmax[:, g % 2, t, i:i + 1], psS[:, bk, c0:c0 + (t + 1) * P], AX, ALU.max)
                        last.then_inc(max_done, 1)
                    elif kind == "P2":
                        m = 4 * s[1] + s[2]
                        dve.wait_ge(exp_done, ONE + b * NH + m + 1)
                        dve.tensor_tensor(p_lo[:, m % 2, :], p_f[:], p_hi[:, m % 2, :], ALU.subtract).then_inc(plow_done, 1)
                    elif kind == "PV":
                        m = 4 * s[1] + s[2]
                        dve.wait_ge(o_full, ONE + b * NH + m + 1)
                        if m == 0:
                            dve.wait_ge(sh_full, ONE + b * NSH)
                        o = psO[:, 0:QT * VW].rearrange("p (t c) -> p t c", t=QT)
                        dve.reciprocal(rsum[:, m % 2, :], o[:, :, 3 * D]).then_inc(o_parts, 1)
                        dve.tensor_reduce(ysum[:], o[:, :, 0:3 * D].rearrange("p t (s d) -> p t d s", s=3), AX, ALU.add).then_inc(o_parts, 1)
                        dve.wait_ge(o_parts, (b * NH + m) * 2 + 2)
                        dve.tensor_tensor(y[:, :, m * D:(m + 1) * D], ysum[:],
                                          rsum[:, m % 2, :].unsqueeze(2).broadcast_to([P, QT, D]), ALU.mult).then_inc(y_done, 1)
                    elif kind == "Y":
                        dve.tensor_tensor(yT_lo[s[1] % 2], bank[bank_of[n]].rearrange("p (k t) -> p k t", k=KC),
                                          yT_hi[s[1] % 2].bitcast(F32), ALU.subtract).then_inc(sh_free, 1)
                    elif kind == "PR":
                        i = s[1]
                        dve.wait_ge(sh_full, ONE + b * NSH + n + 1)
                        dve.wait_ge(xb_ready, b * QT + i + 1)
                        if i == 0:
                            dve.wait_ge(x1_out, ONE + b * 16 * QT)
                        dve.tensor_tensor(z[:, i, :], bank[bank_of[n]], x_res[:, i % 2, :], ALU.add).then_inc(sh_free, 1)
                        dve.wait_ge(sh_free, ONE + b * NSH + n + 1)
                        dve.bn_stats(stats[:, i, :], z[:, i, :]).then_inc(stats_done, 1)
                dve.wait_ge(stats_done, ONE + (b + 1) * QT)
                dve.memset(veps[:], EPS).then_inc(veps_done, 1)
                for i in range(QT):
                    dve.bn_aggr(mv[:, i, :], stats[:, i, :]).then_inc(mv_done, 1)
                dve.wait_ge(mv_done, (b + 1) * QT)
                dve.wait_ge(veps_done, b * 2 + 1)
                dve.tensor_tensor(veps[:], veps[:], mv[:, :, 1], ALU.add).then_inc(veps_done, 1)
                dve.wait_ge(rstd_done, b + 1)
                for i in range(QT):
                    dve.tensor_scalar(z[:, i, :], z[:, i, :], mv[:, i, 0:1], rstd[:, i:i + 1],
                                      ALU.subtract, ALU.mult).then_inc(x1_done, 1)


def bcast(ap, shape, at):
    return ap.unsqueeze(at).broadcast_to(shape)


def products(pe, out, lhs, rhs, chunks):
    n = 0
    for a, c in ((0, 0), (0, 1), (1, 0)):
        for k in range(chunks):
            last = pe.matmul(out, lhs[a](k), rhs[c](k), start=(n == 0), stop=(n == 3 * chunks - 1))
            n += 1
    return last


def expert_phase(nc, sems, tag, x_dram, out_dram, sorted_x, sorted_y, tokens=None, ctx_w=None,
                 router=None, experts=None, shared=None):
    N, C = x_dram.shape
    NT = N // P
    KC = C // P
    chosen = ctx_w is not None
    if chosen:
        E, F, TOP = ctx_w.shape[0], ctx_w.shape[1], 1
    else:
        E, F, TOP = experts[0].shape[0], experts[0].shape[2], 2
    FC = -(-F // P)
    rows = [min(P, F - f * P) for f in range(FC)]
    NS = TOP * NT + E - 1
    NS += 1 - NS % 2
    AHEAD = 4
    BT = 4
    NB = NT // BT
    if not chosen:
        FS = shared[0].shape[1]
        CH = FS // P
        RW = E + 1

    with ExitStack() as outer:
        def sb(name, shape, dt, ctx=outer):
            return ctx.enter_context(nc.sbuf_tensor(f"{tag}_{name}", shape, dt))

        def sem(name):
            return sems.enter_context(nc.semaphore(f"{tag}_{name}"))

        acc = sb("acc", [P, NT, C], F32)
        pos = [sb(f"pos{k}", [P, NT], U32) for k in range(TOP)]
        coef = [sb(f"coef{k}", [P, NT], F32) for k in range(TOP)]
        ident = sb("ident", [P, P], F32)
        table = sb("table", [1, 4, NS + AHEAD], I32)
        t_expert, t_version, t_changed, t_slot = (table[:, r, :] for r in range(4))
        if chosen:
            w_hi = sb("w_hi", [P, E, KC, C], F32R)
            w_lo = sb("w_lo", [P, E, KC, C], F32R)

        with ExitStack() as ctx:
            zeros = sb("zeros", [P, E], F32, ctx)
            iota128 = sb("iota128", [P, NT], F32, ctx)
            iota_s = sb("iota_s", [1, NS + AHEAD], F32, ctx)
            below = sb("below", [P, P], BF16, ctx)
            ones = sb("ones", [P, P], BF16, ctx)
            sel = [sb(f"sel{k}", [P, NT, E], F32, ctx) for k in range(TOP)]
            sel_b = sb("sel_b", [P, NT, E], BF16, ctx)
            pre = sb("pre", [P, NT + 1, E], F32, ctx)
            posf = sb("posf", [P, NT, E], F32, ctx)
            picked = sb("picked", [P, NT, E], F32, ctx)
            picked1 = sb("picked1", [P, NT], F32, ctx)
            more = sb("more", [P, E, NT], F32, ctx)
            ntile = sb("ntile", [P, E], F32, ctx)
            ends = sb("ends", [P, E + 1], F32, ctx)
            base = sb("base", [P, E], F32, ctx)
            some = sb("some", [1, E], F32, ctx)
            past = sb("past", [1, NS + AHEAD, E - 1], F32, ctx)
            tabf = sb("tabf", [1, 3, NS + AHEAD], F32, ctx)
            if chosen:
                tid = sb("tid", [P, NT], I32, ctx)
                above = sb("above", [P, E + 1, NT], F32, ctx)
                craw = sb("craw", [P, 2, KC, C], F32, ctx)
            else:
                xT_hi = sb("xT_hi", [P, KC, N], F32R, ctx)
                xT_lo = sb("xT_lo", [P, KC, N], F32R, ctx)
                wr_raw = sb("wr_raw", [P, KC, RW], F32, ctx)
                wr_hi = sb("wr_hi", [P, KC, RW], F32R, ctx)
                wr_lo = sb("wr_lo", [P, KC, RW], F32R, ctx)
                lgT = sb("lgT", [RW, 512], F32, ctx)
                lg = sb("lg", [P, NT, RW], F32, ctx)
                ex = sb("ex", [P, NT, E], F32, ctx)
                pr = sb("pr", [P, NT, E], F32, ctx)
                row = sb("row", [P, NT], F32, ctx)
                gate = sb("gate", [P, NT], F32, ctx)
                before = sb("before", [P, E, E], F32, ctx)
                rank = sb("rank", [P, NT, E], F32, ctx)
                larger = sb("larger", [P, NT // 2, E, E], F32, ctx)
                same = sb("same", [P, NT // 2, E, E], F32, ctx)
                sraw = sb("sraw", [P, 2, 3, KC * P], F32, ctx)
                s_hi = sb("s_hi", [P, 2, 3, KC * P], F32R, ctx)
                s_lo = sb("s_lo", [P, 2, 3, KC * P], F32R, ctx)
                silu = sb("silu", [P, 512], F32, ctx)
                h_f = sb("h_f", [P, 512], F32, ctx)
                h_hi = sb("h_hi", [P, 2, 512], F32R, ctx)
                h_lo = sb("h_lo", [P, 2, 512], F32R, ctx)

            psT = ctx.enter_context(nc.psum_tensor(f"{tag}_psT", [P, 2, 512], F32))
            psR = ctx.enter_context(nc.psum_tensor(f"{tag}_psR", [P, 512], F32))
            psG = ctx.enter_context(nc.psum_tensor(f"{tag}_psG", [P, 512], F32))
            psU = ctx.enter_context(nc.psum_tensor(f"{tag}_psU", [P, 512], F32))
            psY = ctx.enter_context(nc.psum_tensor(f"{tag}_psY", [P, 2, 512], F32))

            x_in = [sem(f"x_in{q}") for q in range(NB)]
            small_in = sem("small_in")
            raw_in = [sem("raw_in0"), sem("raw_in1")]
            zeroed = sem("zeroed")
            const_done = sem("const_done")
            t_full = sem("t_full")
            t_high = sem("t_high")
            t_free = sem("t_free")
            route = sem("route")
            sel_done = sem("sel_done")
            count_full = sem("count_full")
            pos_done = sem("pos_done")
            table_done = sem("table_done")
            scattered = [sem(f"scattered{q}") for q in range(NB)]
            if not chosen:
                wr_done = sem("wr_done")
                logit_full = sem("logit_full")
                logit_read = sem("logit_read")
                lg_full = sem("lg_full")
                lg_done = sem("lg_done")
                shifted = sem("shifted")
                exp_done = sem("exp_done")
                sh_done = sem("sh_done")
                sl_done = sem("sl_done")
                up_full = sem("up_full")
                silu_done = sem("silu_done")
                hf_done = sem("hf_done")
                hh_done = sem("hh_done")
                hl_done = sem("hl_done")
                y_full = sem("y_full")
                y_added = sem("y_added")
            block = ctx.enter_context(nc.Block())

            def chunks(eng, body):
                body(0, 0)
                with eng.Fori(0, (CH - 1) // 2) as t:
                    body(t, 1)
                    body(t, 2)

            @block.sync
            def _(sp):
                if chosen:
                    sp.dma_start(tid[:], tokens.rearrange("(t p) -> p t", p=P),
                                 allow_slow_non_contiguous=True).then_inc(small_in, 16)
                    for e in range(2):
                        sp.dma_start(craw[:, e], ctx_w[e].rearrange("(k p) f -> p k f", p=P)).then_inc(raw_in[e], 16)
                for q in range(NB):
                    sp.dma_start(acc[:, q * BT:(q + 1) * BT, :],
                                 x_dram[q * BT * P:(q + 1) * BT * P, :].rearrange("(t p) c -> p t c", p=P)).then_inc(x_in[q], 16)
                if chosen:
                    for e in range(2, E):
                        sp.wait_ge(t_full, (e - 1) * KC)
                        sp.dma_start(craw[:, e % 2], ctx_w[e].rearrange("(k p) f -> p k f", p=P)).then_inc(raw_in[e % 2], 16)
                else:
                    sp.dma_start(wr_raw[:, :, 0:E], router[0].rearrange("(k p) e -> p k e", p=P)).then_inc(small_in, 16)
                    sp.dma_start(wr_raw[:, :, E:RW], router[1].rearrange("(k p) e -> p k e", p=P),
                                 allow_slow_non_contiguous=True).then_inc(small_in, 16)

                    def load(n, slot):
                        for m in range(2):
                            sp.dma_start(sraw[:, slot, m, :].rearrange("p (k n) -> p k n", k=KC),
                                         shared[m][:, bass.ds(n * P, P)].rearrange("(k p) n -> p k n", p=P)).then_inc(raw_in[slot], 16)
                        sp.dma_start(sraw[:, slot, 2, :], shared[2][bass.ds(n * P, P), :]).then_inc(raw_in[slot], 16)

                    def body(t, c):
                        n = (2 * t + c + 1) % CH
                        sp.wait_ge(sl_done, ONE + 2 * t + c)
                        load(n, (c + 1) % 2)

                    load(0, 0)
                    chunks(sp, body)

            @block.gpsimd
            def _(pool):
                if not chosen:
                    for s in (hf_done, y_added, y_full, hh_done, hl_done, sl_done):
                        pool.sem_inc(s, ONE)
                pool.memset(ident[:], 0.0).then_inc(zeroed, 1)
                pool.memset(below[:], 1.0).then_inc(zeroed, 1)
                pool.memset(ones[:], 1.0).then_inc(const_done, 1)
                pool.iota(iota128[:], pattern=[[P, NT]], base=0, channel_multiplier=0,
                          allow_small_or_imprecise_dtypes=True).then_inc(const_done, 1)
                pool.iota(iota_s[:], pattern=[[1, NS + AHEAD]], base=0, channel_multiplier=0,
                          allow_small_or_imprecise_dtypes=True).then_inc(const_done, 1)
                pool.wait_ge(zeroed, 2)
                pool.affine_select(out=ident[:], in_=ident[:], compare_op=ALU.not_equal, fill=1.0, base=0,
                                   pattern=[[-1, P]], channel_multiplier=1).then_inc(const_done, 1)
                pool.affine_select(out=below[:], in_=below[:], compare_op=ALU.is_gt, fill=0.0, base=0,
                                   pattern=[[1, P]], channel_multiplier=-1).then_inc(const_done, 1)
                if not chosen:
                    pool.memset(before[:], 1.0).then_inc(zeroed, 1)
                    pool.wait_ge(zeroed, 3)
                    pool.affine_select(out=before[:], in_=before[:], compare_op=ALU.is_gt, fill=0.0, base=0,
                                       pattern=[[1, E], [-1, E]], channel_multiplier=0).then_inc(const_done, 1)
                pool.wait_ge(pos_done, TOP)
                for q in range(NB):
                    pool.wait_ge(x_in[q], 16)
                for t in range(NT):
                    for k in range(TOP):
                        pool.indirect_dma_start(out=sorted_x, out_offset=bass.IndirectOffsetOnAxis(ap=pos[k][:, t:t + 1], axis=0),
                                                in_=acc[:, t, :], in_offset=None).then_inc(scattered[t // BT], 16)
                for q in range(NB):
                    pool.wait_ge(scattered[q], 16 * BT * TOP)

            @block.tensor
            def _(pe):
                def counts(pe):
                    pe.wait_ge(sel_done, 1)
                    s = sel_b[:].rearrange("p t e -> p (t e)")
                    pe.matmul(psR[:, 0:NT * E], below[:], s, start=True, stop=True)
                    pe.matmul(psR[:, 256:256 + NT * E], ones[:], s, start=True, stop=True).then_inc(count_full, 1)

                pe.wait_ge(const_done, 5)
                if chosen:
                    for e in range(E):
                        pe.wait_ge(raw_in[e % 2], 16 * (e // 2 + 1))
                        for k in range(KC):
                            n = e * KC + k
                            if n >= 2:
                                pe.wait_ge(t_free, n - 1)
                            for c in range(KC):
                                last = pe.transpose(psT[:, n % 2, c * P:(c + 1) * P], craw[:, e % 2, k, c * P:(c + 1) * P], ident[:])
                            last.then_inc(t_full, 1)
                        if e == 1:
                            counts(pe)
                else:
                    for t in range(NT):
                        if t % BT == 0:
                            pe.wait_ge(x_in[t // BT], 16)
                        if t >= 2:
                            pe.wait_ge(t_free, t - 1)
                        for k in range(KC):
                            last = pe.transpose(psT[:, t % 2, k * P:(k + 1) * P], acc[:, t, k * P:(k + 1) * P], ident[:])
                        last.then_inc(t_full, 1)
                    pe.wait_ge(wr_done, 2)
                    pe.wait_ge(t_free, NT)
                    for q in range(NB):
                        if q:
                            pe.wait_ge(logit_read, q)
                        products(pe, psG[0:RW, :], [lambda k: wr_hi[:, k, :], lambda k: wr_lo[:, k, :]],
                                 [lambda k: xT_hi[:, k, q * 512:(q + 1) * 512], lambda k: xT_lo[:, k, q * 512:(q + 1) * 512]],
                                 KC).then_inc(logit_full, 1)
                        pe.wait_ge(logit_read, q + 1)
                        if q:
                            pe.wait_ge(lg_done, q)
                        for i in range(BT):
                            last = pe.transpose(psR[:, i * RW:(i + 1) * RW], lgT[:, i * P:(i + 1) * P], ident[0:RW, 0:RW])
                        last.then_inc(lg_full, 1)
                    pe.wait_ge(lg_done, NB)

                    gates, ups = [psG, psT[:, 0, :]], [psU, psT[:, 1, :]]

                    def up(t, c, q):
                        slot, g = c % 2, c * NB + q
                        pe.wait_ge(hf_done, ONE + t * 2 * NB + max(g - 1, 0))
                        xs = [lambda k: xT_hi[:, k, q * 512:(q + 1) * 512], lambda k: xT_lo[:, k, q * 512:(q + 1) * 512]]
                        for m, bank in ((0, gates[g % 2]), (1, ups[g % 2])):
                            last = products(pe, bank[:, :], [lambda k: s_hi[:, slot, m, k * P:(k + 1) * P],
                                                             lambda k: s_lo[:, slot, m, k * P:(k + 1) * P]], xs, KC)
                        last.then_inc(up_full, 1)

                    def down(t, c, q):
                        slot, g = c % 2, c * NB + q
                        pe.wait_ge(hl_done, ONE + t * 2 * NB + g + 1)
                        for i in range(BT):
                            m = g * BT + i
                            pe.wait_ge(y_added, ONE + t * 2 * NT + max(m - 1, 0))
                            products(pe, psY[:, m % 2, :], [lambda k: h_hi[:, g % 2, i * P:(i + 1) * P], lambda k: h_lo[:, g % 2, i * P:(i + 1) * P]],
                                     [lambda k: s_hi[:, slot, 2, :], lambda k: s_lo[:, slot, 2, :]], 1).then_inc(y_full, 1)

                    def body(t, c):
                        pe.wait_ge(sl_done, ONE + 2 * t + c + 1)
                        for q in range(NB):
                            up(t, c, q)
                            if q:
                                down(t, c, q - 1)
                            elif c:
                                down(t, c - 1, NB - 1)

                    counts(pe)
                    chunks(pe, body)
                    down((CH - 1) // 2, 0, NB - 1)

            @block.scalar
            def _(act):
                if chosen:
                    for n in range(E * KC):
                        e, k = n // KC, n % KC
                        act.wait_ge(t_full, n + 1)
                        act.copy(w_hi[:, e, :, k * P:(k + 1) * P], psT[:, n % 2, :].rearrange("p (c n) -> p c n", c=KC)).then_inc(t_high, 1)
                    return
                for t in range(NT):
                    act.wait_ge(t_full, t + 1)
                    act.copy(xT_hi[:, :, t * P:(t + 1) * P], psT[:, t % 2, :].rearrange("p (k n) -> p k n", k=KC)).then_inc(t_high, 1)
                act.wait_ge(small_in, 32)
                act.copy(wr_hi[:], wr_raw[:]).then_inc(wr_done, 1)
                act.wait_ge(shifted, 1)
                act.activation(ex[:], ex[:], ACT.Exp).then_inc(exp_done, 1)
                act.activation(gate[:], lg[:, :, E], ACT.Exp, scale=-1.0).then_inc(exp_done, 1)

                def high_w(t, c):
                    slot = c % 2
                    act.wait_ge(raw_in[slot], 48 * (t + c // 2 + 1))
                    act.copy(s_hi[:, slot], sraw[:, slot]).then_inc(sh_done, 1)

                def body(t, c):
                    for q in range(NB):
                        g = c * NB + q
                        act.wait_ge(up_full, t * 2 * NB + g + 1)
                        act.wait_ge(hf_done, ONE + t * 2 * NB + g)
                        act.activation(silu[:], gates[g % 2][:, :], ACT.Silu).then_inc(silu_done, 1)
                        act.wait_ge(hf_done, ONE + t * 2 * NB + g + 1)
                        act.wait_ge(y_full, ONE + t * 2 * NT + max(g - 1, 0) * BT)
                        act.copy(h_hi[:, g % 2, :], h_f[:]).then_inc(hh_done, 1)
                        if q == 2:
                            act.wait_ge(y_full, ONE + (2 * t + c) * NT)
                            high_w(t, c + 1)

                gates = [psG, psT[:, 0, :]]
                high_w(0, 0)
                chunks(act, body)

            @block.vector
            def _(dve):
                step = [0]

                def then(ins):
                    step[0] += 1
                    ins.then_inc(route, 1)
                    dve.wait_ge(route, step[0])

                if chosen:
                    def split(n):
                        e, k = n // KC, n % KC
                        dve.wait_ge(t_high, n + 1)
                        dve.tensor_tensor(w_lo[:, e, :, k * P:(k + 1) * P], psT[:, n % 2, :].rearrange("p (c n) -> p c n", c=KC),
                                          w_hi[:, e, :, k * P:(k + 1) * P].bitcast(F32), ALU.subtract).then_inc(t_free, 1)
                    dve.wait_ge(small_in, 16)
                    dve.memset(above[:, 0, :], 1.0)
                    dve.memset(above[:, E, :], 0.0)
                    for e in range(1, E):
                        last = dve.tensor_scalar(above[:, e, :], tid[:], float(25000 // E * e), None, ALU.is_ge)
                    then(last)
                    then(dve.tensor_tensor(sel[0][:].rearrange("p t e -> p e t"), above[:, 0:E, :], above[:, 1:E + 1, :], ALU.subtract))
                    dve.tensor_copy(sel_b[:], sel[0][:]).then_inc(sel_done, 1)
                    for n in range(2 * KC):
                        split(n)
                else:
                    for t in range(NT):
                        dve.wait_ge(t_high, t + 1)
                        dst = (slice(None), slice(None), slice(t * P, (t + 1) * P))
                        dve.tensor_tensor(xT_lo[dst], psT[:, t % 2, :].rearrange("p (k n) -> p k n", k=KC), xT_hi[dst].bitcast(F32),
                                          ALU.subtract).then_inc(t_free, 1)
                    dve.wait_ge(wr_done, 1)
                    dve.tensor_tensor(wr_lo[:], wr_raw[:], wr_hi[:].bitcast(F32), ALU.subtract).then_inc(wr_done, 1)
                    for q in range(NB):
                        dve.wait_ge(logit_full, q + 1)
                        if q:
                            dve.wait_ge(lg_full, q)
                        dve.tensor_copy(lgT[:], psG[0:RW, :]).then_inc(logit_read, 1)
                        dve.wait_ge(lg_full, q + 1)
                        dve.tensor_copy(lg[:, q * BT:(q + 1) * BT, :], psR[:, 0:BT * RW].rearrange("p (t e) -> p t e", t=BT)).then_inc(lg_done, 1)
                    dve.wait_ge(lg_done, NB)
                    full = [P, NT, E]
                    then(dve.tensor_reduce(row[:], lg[:, :, 0:E], AX, ALU.max))
                    dve.tensor_tensor(ex[:], lg[:, :, 0:E], bcast(row[:], full, 2), ALU.subtract).then_inc(shifted, 1)
                    dve.wait_ge(exp_done, 2)
                    then(dve.tensor_reduce(row[:], ex[:], AX, ALU.add))
                    then(dve.reciprocal(row[:], row[:]))
                    then(dve.tensor_tensor(pr[:], ex[:], bcast(row[:], full, 2), ALU.mult))
                    then(dve.tensor_scalar(gate[:], gate[:], 1.0, None, ALU.add))
                    then(dve.reciprocal(gate[:], gate[:]))
                    dve.wait_ge(const_done, 6)
                    HT = NT // 2
                    quad = [P, HT, E, E]
                    for hf in range(2):
                        half = pr[:, hf * HT:(hf + 1) * HT, :]
                        own, other = bcast(half, quad, 3), bcast(half, quad, 2)
                        dve.tensor_tensor(larger[:], other, own, ALU.is_gt)
                        then(dve.tensor_tensor(same[:], other, own, ALU.is_equal))
                        then(dve.tensor_tensor(same[:], same[:], bcast(before[:], quad, 1), ALU.mult))
                        then(dve.tensor_tensor(larger[:], larger[:], same[:], ALU.add))
                        then(dve.tensor_reduce(rank[:, hf * HT:(hf + 1) * HT, :], larger[:], AX, ALU.add))
                    dve.tensor_scalar(sel_b[:], rank[:], float(TOP), None, ALU.is_lt).then_inc(sel_done, 1)
                    for k in range(TOP):
                        then(dve.tensor_scalar(sel[k][:], rank[:], float(k), None, ALU.is_equal))
                        then(dve.tensor_tensor(picked[:], sel[k][:], pr[:], ALU.mult))
                        then(dve.tensor_reduce(coef[k][:], picked[:], AX, ALU.add))

                dve.wait_ge(const_done, 5)
                dve.wait_ge(count_full, 1)
                within = psR[:, 0:NT * E].rearrange("p (t e) -> p t e", t=NT)
                total = psR[:, 256:256 + NT * E].rearrange("p (t e) -> p t e", t=NT)
                then(dve.memset(pre[:, 0, :], 0.0))
                for t in range(NT):
                    then(dve.tensor_tensor(pre[:, t + 1, :], total[:, t, :], pre[:, t, :], ALU.add))
                full = [P, E, NT]
                then(dve.tensor_tensor(more[:], bcast(pre[:, NT, :], full, 2), bcast(iota128[:], full, 1), ALU.is_gt))
                then(dve.tensor_reduce(ntile[:], more[:], AX, ALU.add))
                then(dve.memset(ends[:, 0:1], 0.0))
                for e in range(E):
                    then(dve.tensor_tensor(ends[:, e + 1:e + 2], ends[:, e:e + 1], ntile[:, e:e + 1], ALU.add))
                then(dve.tensor_scalar(base[:], ends[:, 0:E], float(P), None, ALU.mult))
                full = [P, NT, E]
                then(dve.tensor_tensor(posf[:], within, pre[:, 0:NT, :], ALU.add))
                then(dve.tensor_tensor(posf[:], posf[:], bcast(base[:], full, 1), ALU.add))
                for k in range(TOP):
                    then(dve.tensor_tensor(picked[:], posf[:], sel[k][:], ALU.mult))
                    then(dve.tensor_reduce(picked1[:], picked[:], AX, ALU.add))
                    then(dve.tensor_copy(pos[k][:], picked1[:]))
                    dve.sem_inc(pos_done, 1)
                full = [1, NS + AHEAD, E - 1]
                then(dve.tensor_scalar(some[:], ntile[0:1, :], 0.0, None, ALU.is_gt))
                then(dve.tensor_tensor(past[:], bcast(iota_s[:], full, 2), bcast(ends[0:1, 1:E], full, 1), ALU.is_ge))
                then(dve.tensor_reduce(tabf[:, 0, :], past[:], AX, ALU.add))
                then(dve.tensor_tensor(past[:], past[:], bcast(some[:, 0:E - 1], full, 1), ALU.mult))
                then(dve.tensor_reduce(tabf[:, 1, :], past[:], AX, ALU.add))
                dve.tensor_copy(table[:, 0:2, :], tabf[:, 0:2, :])
                dve.memset(table[:, 2, 0:1], 1)
                dve.memset(table[:, 2, NS:NS + AHEAD], 0)
                then(dve.tensor_tensor(table[:, 2, 1:NS], tabf[:, 1, 1:NS], tabf[:, 1, 0:NS - 1], ALU.subtract))
                then(dve.tensor_scalar(tabf[:, 2, :], tabf[:, 1, :], 3.0, -3.0, ALU.is_ge, ALU.mult))
                then(dve.tensor_tensor(tabf[:, 2, :], tabf[:, 2, :], tabf[:, 1, :], ALU.add))
                then(dve.tensor_scalar(tabf[:, 1, :], tabf[:, 1, :], 6.0, -3.0, ALU.is_ge, ALU.mult))
                then(dve.tensor_tensor(table[:, 3, :], tabf[:, 2, :], tabf[:, 1, :], ALU.add))
                if chosen:
                    for n in range(2 * KC, E * KC):
                        split(n)
                    return

                ups = [psU, psT[:, 1, :]]

                def low_w(t, c):
                    slot = c % 2
                    dve.wait_ge(sh_done, 2 * t + c + 1)
                    dve.tensor_tensor(s_lo[:, slot], sraw[:, slot], s_hi[:, slot].bitcast(F32), ALU.subtract).then_inc(sl_done, 1)

                def body(t, c):
                    for q in range(NB):
                        g = c * NB + q
                        done = t * 2 * NB + g
                        dve.wait_ge(silu_done, done + 1)
                        dve.wait_ge(hl_done, ONE + done)
                        dve.tensor_tensor(h_f[:], ups[g % 2][:, :], silu[:], ALU.mult).then_inc(hf_done, 1)
                        if q:
                            add(t, c, q - 1)
                        elif c:
                            add(t, c - 1, NB - 1)
                        dve.wait_ge(hh_done, ONE + done + 1)
                        dve.tensor_tensor(h_lo[:, g % 2, :], h_f[:], h_hi[:, g % 2, :].bitcast(F32), ALU.subtract).then_inc(hl_done, 1)
                        if q == 2:
                            low_w(t, c + 1)

                def add(t, c, q):
                    dve.wait_ge(scattered[q], 16 * BT * TOP)
                    for i in range(BT):
                        tok = q * BT + i
                        m = (c * NB + q) * BT + i
                        dve.wait_ge(y_full, ONE + t * 2 * NT + m + 1)
                        dve.scalar_tensor_tensor(acc[:, tok, :], psY[:, m % 2, :], gate[:, tok:tok + 1], acc[:, tok, :],
                                                 ALU.mult, ALU.add).then_inc(y_added, 1)

                low_w(0, 0)
                chunks(dve, body)
                add((CH - 1) // 2, 0, NB - 1)

        with ExitStack() as ctx:
            xs = sb("xs", [P, 2, C], F32, ctx)
            xsT_hi = [sb(f"xsT_hi{s}", [P, KC, P], F32R, ctx) for s in range(2)]
            xsT_lo = [sb(f"xsT_lo{s}", [P, KC, P], F32R, ctx) for s in range(2)]
            silu = sb("silu_s", [P, F], F32, ctx)
            h_f = sb("h_s", [P, 2, F], F32, ctx)
            hT_hi = [sb(f"hT_hi{s}", [P, FC, P], F32R, ctx) for s in range(2)]
            hT_lo = [sb(f"hT_lo{s}", [P, FC, P], F32R, ctx) for s in range(2)]
            y_sb = sb("y_sb", [P, 2, C], F32, ctx)
            got = sb("got", [P, 4, C], F32, ctx)
            stats = sb("stats", [P, NT, 6], F32, ctx)
            mv = sb("mv", [P, NT, 2], F32, ctx)
            veps = sb("veps", [P, NT], F32, ctx)
            powm = sb("powm", [P, NT], F32, ctx)
            rstd = sb("rstd", [P, NT], F32, ctx)
            if not chosen:
                WG, WD = KC * F, FC * C
                WALL = 2 * WG + WD
                wraw = sb("wraw", [P, WALL], F32, ctx)
                wv_hi = sb("wv_hi", [P, 3, WALL], F32R, ctx)
                wv_lo = sb("wv_lo", [P, 3, WALL], F32R, ctx)
            psX = ctx.enter_context(nc.psum_tensor(f"{tag}_psX", [P, 2, 512], F32))
            psG = ctx.enter_context(nc.psum_tensor(f"{tag}_psG2", [P, 2, 512], F32))
            psU = ctx.enter_context(nc.psum_tensor(f"{tag}_psU2", [P, 2, 512], F32))
            psH = ctx.enter_context(nc.psum_tensor(f"{tag}_psH", [P, 512], F32))
            psY = ctx.enter_context(nc.psum_tensor(f"{tag}_psY2", [P, 512], F32))

            xs_in = [sem("xs_in0"), sem("xs_in1")]
            init_done = sem("init_done")
            xT_full = sem("xT_full")
            xhigh_done = sem("xhigh_done")
            xlow_done = sem("xlow_done")
            up_full = sem("up_full2")
            silu_done = sem("silu_done2")
            h_done = sem("h_done")
            hT_full = sem("hT_full")
            hhigh_done = sem("hhigh_done")
            hlow_done = sem("hlow_done")
            y_full = sem("y_full2")
            y_copied = sem("y_copied")
            y_stored = [sem("y_stored0"), sem("y_stored1")]
            got_in = [sem(f"got_in{r}") for r in range(4)]
            added = sem("added")
            stats_done = sem("stats_done")
            mv_done = sem("mv_done")
            veps_done = sem("veps_done")
            rstd_done = sem("rstd_done")
            out_done = sem("out_done")
            stored = sem("stored")
            if not chosen:
                wraw_in = sem("wraw_in")
                whigh_done = sem("whigh_done")
                wlow_done = sem("wlow_done")
            block = ctx.enter_context(nc.Block())

            def tiles(eng, body):
                body(0, 0, 0)
                with eng.Fori(0, (NS - 1) // 2) as t:
                    body(2 * t + 1, t, 1)
                    body(2 * t + 2, t, 2)

            def entry(eng, row, s, high):
                return eng.value_load(row[0:1, bass.ds(s, 1)], min_val=0, max_val=high)

            full = F // P

            @block.sync
            def _(sp):
                def load_x(s, t, c):
                    sp.dma_start(xs[:, c % 2, :], sorted_x[bass.ds(s * P, P), :]).then_inc(xs_in[c % 2], 16)

                def load_w(e):
                    sp.dma_start(wraw[:, 0:WG].rearrange("p (k f) -> p k f", k=KC),
                                 experts[0][bass.ds(e, 1)].rearrange("a (k p) f -> p (a k) f", p=P)).then_inc(wraw_in, 16)
                    sp.dma_start(wraw[:, WG:2 * WG].rearrange("p (k f) -> p k f", k=KC),
                                 experts[1][bass.ds(e, 1)].rearrange("a (k p) f -> p (a k) f", p=P)).then_inc(wraw_in, 16)
                    down = wraw[:, 2 * WG:WALL].rearrange("p (k c) -> p k c", k=FC)
                    sp.dma_start(down[:, 0:full, :], experts[2][bass.ds(e, 1), 0:full * P, :]
                                 .rearrange("a (k p) c -> p (a k) c", p=P)).then_inc(wraw_in, 16)
                    sp.dma_start(down[0:rows[-1], full, :], experts[2][bass.ds(e, 1), full * P:F, :]
                                 .rearrange("a p c -> p (a c)")).then_inc(wraw_in, 16)

                def entries(s):
                    if chosen:
                        return None
                    return entry(sp, t_changed, s, 1), entry(sp, t_version, s, E - 1), entry(sp, t_expert, s, E - 1)

                def weights(found):
                    if chosen:
                        return
                    changed, version, e = found
                    with sp.If(changed > 0):
                        sp.wait_ge(wlow_done, ONE + version)
                        load_w(e)

                if not chosen:
                    sp.wait_ge(init_done, 3)
                load_x(0, 0, 0)
                weights(entries(0))
                load_x(1, 0, 1)
                for s in (1, 2):
                    weights(entries(s))

                def body(s, t, c):
                    found = entries(s + 3)
                    sp.wait_ge(xT_full, s + 1)
                    load_x(s + 2, t, c)
                    if c:
                        sp.wait_ge(y_copied, ONE + s)
                        sp.dma_start(sorted_y[bass.ds((s - 1) * P, P), :], y_sb[:, (c - 1) % 2, :]).then_inc(y_stored[(c - 1) % 2], 16)
                    weights(found)

                tiles(sp, body)
                sp.wait_ge(y_copied, ONE + NS)
                sp.dma_start(sorted_y[(NS - 1) * P:NS * P, :], y_sb[:, (NS - 1) % 2, :]).then_inc(y_stored[(NS - 1) % 2], 16)
                sp.wait_ge(xs_in[0], 16 * ((NS + 3) // 2))
                sp.wait_ge(xs_in[1], 16 * ((NS + 2) // 2))
                for q in range(NT):
                    sp.wait_ge(out_done, q + 1)
                    sp.dma_start(out_dram[q * P:(q + 1) * P, :], acc[:, q, :]).then_inc(stored, 16)
                sp.wait_ge(stored, 16 * NT)

            @block.gpsimd
            def _(pool):
                for s in (y_copied, xlow_done, h_done, hlow_done, hT_full, up_full, y_full, *y_stored):
                    pool.sem_inc(s, ONE)
                if not chosen:
                    pool.sem_inc(wlow_done, ONE)
                if not chosen:
                    pool.memset(wraw[rows[-1]:P, WALL - C:WALL], 0.0).then_inc(init_done, 1)
                pool.wait_ge(y_stored[0], ONE + 16 * ((NS + 1) // 2))
                pool.wait_ge(y_stored[1], ONE + 16 * (NS // 2))
                for t in range(NT):
                    for k in range(TOP):
                        n = t * TOP + k
                        if n >= 4:
                            pool.wait_ge(added, n - 3)
                        pool.indirect_dma_start(out=got[:, n % 4, :], out_offset=None, in_=sorted_y,
                                                in_offset=bass.IndirectOffsetOnAxis(ap=pos[k][:, t:t + 1], axis=0)).then_inc(got_in[n % 4], 16)
                pool.wait_ge(init_done, 2)
                pool.wait_ge(veps_done, 1)
                pool.tensor_tensor(rstd[:], veps[:], powm[:], ALU.pow).then_inc(rstd_done, 1)

            @block.tensor
            def _(pe):
                pe.wait_ge(init_done, 2 if chosen else 3)

                def turn_x(s, t, c):
                    pe.wait_ge(xs_in[c % 2], 16 * (t + c // 2 + 1))
                    pe.wait_ge(xlow_done, ONE + s - 1 if c else ONE)
                    for k in range(KC):
                        last = pe.transpose(psX[:, c % 2, k * P:(k + 1) * P], xs[:, c % 2, k * P:(k + 1) * P], ident[:])
                    last.then_inc(xT_full, 1)

                def moving(s):
                    if chosen:
                        e = entry(pe, t_expert, s, E - 1)
                        both = [lambda k, w=w: w[:, bass.ds(e, 1), k, :].rearrange("p a n -> p (a n)") for w in (w_hi, w_lo)]
                        return both, both, both
                    b = entry(pe, t_slot, s, 2)
                    def part(at, width):
                        return [lambda k, w=w: w[:, bass.ds(b, 1), at + k * width:at + (k + 1) * width].rearrange("p a n -> p (a n)")
                                for w in (wv_hi, wv_lo)]
                    down = [lambda k, w=w: w[0:rows[k], bass.ds(b, 1), 2 * WG + k * C:2 * WG + (k + 1) * C].rearrange("p a n -> p (a n)")
                            for w in (wv_hi, wv_lo)]
                    return part(0, F), part(WG, F), down

                def up(s, t, c):
                    gate_w, up_w, _ = moving(s)
                    if not chosen:
                        version = entry(pe, t_version, s, E - 1)
                        pe.wait_ge(wlow_done, ONE + version + 1)
                    pe.wait_ge(xlow_done, ONE + s + 1)
                    pe.wait_ge(h_done, ONE + s - 1 if c else ONE)
                    x = [lambda k: xsT_hi[c % 2][:, k, :], lambda k: xsT_lo[c % 2][:, k, :]]
                    last = products(pe, psG[:, c % 2, 0:F], x, gate_w, KC)
                    if not chosen:
                        last = products(pe, psU[:, c % 2, 0:F], x, up_w, KC)
                    last.then_inc(up_full, 1)

                def down(s, t, c):
                    _, _, down_w = moving(s)
                    pe.wait_ge(hlow_done, ONE + s + 1)
                    pe.wait_ge(y_copied, ONE + s)
                    h = [lambda k: hT_hi[c % 2][0:rows[k], k, :], lambda k: hT_lo[c % 2][0:rows[k], k, :]]
                    products(pe, psY[:, :], h, down_w, FC).then_inc(y_full, 1)

                def turn_h(s, t, c):
                    pe.wait_ge(h_done, ONE + s + 1)
                    pe.wait_ge(hlow_done, ONE + s)
                    for k in range(FC):
                        last = pe.transpose(psH[0:rows[k], k * P:(k + 1) * P], h_f[:, c % 2, k * P:k * P + rows[k]], ident[:])
                    last.then_inc(hT_full, 1)

                def body(s, t, c):
                    up(s, t, c)
                    turn_x(s + 1, t, c + 1)
                    if c:
                        down(s - 1, t, c - 1)
                    turn_h(s, t, c)

                turn_x(0, 0, 0)
                tiles(pe, body)
                down(NS - 1, 0, NS - 1)

            @block.scalar
            def _(act):
                def high_x(s, t, c):
                    act.wait_ge(xT_full, s + 1)
                    if c:
                        act.wait_ge(up_full, ONE + s - 1)
                    act.copy(xsT_hi[c % 2][:], psX[:, c % 2, :].rearrange("p (k n) -> p k n", k=KC)).then_inc(xhigh_done, 1)

                def split_w(s):
                    if chosen:
                        return
                    changed = entry(act, t_changed, s, 1)
                    version = entry(act, t_version, s, E - 1)
                    b = entry(act, t_slot, s, 2)
                    with act.If(changed > 0):
                        act.wait_ge(wraw_in, version * 64 + 64)
                        act.copy(wv_hi[:, bass.ds(b, 1), :].rearrange("p a n -> p (a n)"), wraw[:]).then_inc(whigh_done, 1)

                def copy_y(s, t, c):
                    act.wait_ge(y_full, ONE + s + 1)
                    act.wait_ge(y_stored[c % 2], ONE + 16 * t)
                    act.copy(y_sb[:, c % 2, :], psY[:]).then_inc(y_copied, 1)

                def body(s, t, c):
                    act.wait_ge(up_full, ONE + s + 1)
                    act.wait_ge(h_done, ONE + s)
                    act.activation(silu[:], psG[:, c % 2, 0:F], ACT.Silu).then_inc(silu_done, 1)
                    high_x(s + 1, t, c + 1)
                    if c:
                        copy_y(s - 1, t, c - 1)
                    act.wait_ge(hT_full, ONE + s + 1)
                    if c:
                        act.wait_ge(y_full, ONE + s - 1)
                    if chosen:
                        act.copy(hT_hi[c % 2][:], psH[:].rearrange("p (k n) -> p k n", k=FC)).then_inc(hhigh_done, 1)
                    else:
                        act.copy(hT_hi[c % 2][:], psH[:, 0:FC * P].rearrange("p (k n) -> p k n", k=FC)).then_inc(hhigh_done, 1)
                    split_w(s + 2)

                split_w(0)
                split_w(1)
                high_x(0, 0, 0)
                tiles(act, body)
                copy_y(NS - 1, (NS - 1) // 2, 0)

            @block.vector
            def _(dve):
                dve.memset(psH[:], 0.0).then_inc(init_done, 1)
                dve.memset(powm[:], -0.5).then_inc(init_done, 1)

                def low_x(s, t, c):
                    dve.wait_ge(xhigh_done, s + 1)
                    dve.tensor_tensor(xsT_lo[c % 2][:], psX[:, c % 2, :].rearrange("p (k n) -> p k n", k=KC),
                                      xsT_hi[c % 2][:].bitcast(F32), ALU.subtract).then_inc(xlow_done, 1)

                def split_w(s):
                    if chosen:
                        return
                    changed = entry(dve, t_changed, s, 1)
                    version = entry(dve, t_version, s, E - 1)
                    b = entry(dve, t_slot, s, 2)
                    with dve.If(changed > 0):
                        dve.wait_ge(whigh_done, version + 1)
                        dve.tensor_tensor(wv_lo[:, bass.ds(b, 1), :].rearrange("p a n -> p (a n)"), wraw[:],
                                          wv_hi[:, bass.ds(b, 1), :].rearrange("p a n -> p (a n)").bitcast(F32), ALU.subtract).then_inc(wlow_done, 1)

                def body(s, t, c):
                    dve.wait_ge(silu_done, s + 1)
                    dve.wait_ge(hT_full, ONE + s - 1 if c else ONE)
                    dve.tensor_tensor(h_f[:, c % 2, :], (psG if chosen else psU)[:, c % 2, 0:F], silu[:], ALU.mult).then_inc(h_done, 1)
                    low_x(s + 1, t, c + 1)
                    dve.wait_ge(hhigh_done, s + 1)
                    dve.tensor_tensor(hT_lo[c % 2][:], psH[:, 0:FC * P].rearrange("p (k n) -> p k n", k=FC),
                                      hT_hi[c % 2][:].bitcast(F32), ALU.subtract).then_inc(hlow_done, 1)
                    split_w(s + 2)

                split_w(0)
                split_w(1)
                low_x(0, 0, 0)
                tiles(dve, body)

                for t in range(NT):
                    for k in range(TOP):
                        n = t * TOP + k
                        dve.wait_ge(got_in[n % 4], 16 * (n // 4 + 1))
                        if k:
                            dve.wait_ge(added, n)
                        if chosen:
                            dve.tensor_tensor(acc[:, t, :], acc[:, t, :], got[:, n % 4, :], ALU.add).then_inc(added, 1)
                        else:
                            dve.scalar_tensor_tensor(acc[:, t, :], got[:, n % 4, :], coef[k][:, t:t + 1], acc[:, t, :],
                                                     ALU.mult, ALU.add).then_inc(added, 1)
                    dve.wait_ge(added, (t + 1) * TOP)
                    dve.bn_stats(stats[:, t, :], acc[:, t, :]).then_inc(stats_done, 1)
                dve.wait_ge(stats_done, NT)
                for q in range(NT):
                    dve.bn_aggr(mv[:, q, :], stats[:, q, :]).then_inc(mv_done, 1)
                dve.wait_ge(mv_done, NT)
                dve.tensor_scalar(veps[:], mv[:, :, 1], EPS, None, ALU.add).then_inc(veps_done, 1)
                dve.wait_ge(rstd_done, 1)
                for q in range(NT):
                    dve.tensor_scalar(acc[:, q, :], acc[:, q, :], mv[:, q, 0:1], rstd[:, q:q + 1], ALU.subtract, ALU.mult).then_inc(out_done, 1)


def decoder_kernel(nc, x, itok, ctx_w, w_attn, b_attn, w_proj, b_proj, wr, wg, wu, wd, sg, su, sd, wsg, out):
    B, T, C = x.shape
    tiles1, tiles2 = B * T // P + 3 + 2, 2 * (B * T // P) + 7 + 2

    def scratch(name, rows):
        return nc.dram_tensor(name, [rows, C], F32, kind="Internal").ap()

    x1, x2 = scratch("x1", B * T), scratch("x2", B * T)
    sx1, sy1 = scratch("sorted_x1", tiles1 * P), scratch("sorted_y1", (tiles1 - 2) * P)
    sx2, sy2 = scratch("sorted_x2", tiles2 * P), scratch("sorted_y2", (tiles2 - 2) * P)
    with ExitStack() as sems:
        attention_phase(nc, sems, x, w_attn, b_attn, w_proj, b_proj, x1.rearrange("(b t) c -> b t c", b=B), (sx1, sx2))
        expert_phase(nc, sems, "chosen", x1, x2, sx1, sy1, tokens=itok.rearrange("b s -> (b s)"), ctx_w=ctx_w)
        expert_phase(nc, sems, "routed", x2, out.rearrange("b s d -> (b s) d"), sx2, sy2,
                     router=(wr, wsg), experts=(wg, wu, wd), shared=(sg, su, sd))


_INS = ["x", "itok_BxS_13_99985", "ctx_2048", "L0_attn_w_attn", "L0_attn_b_attn", "L0_attn_w_proj", "L0_attn_b_proj",
        "L0_ffn_Wr", "L0_ffn_Wg", "L0_ffn_Wu", "L0_ffn_Wd", "L0_ffn_Sg", "L0_ffn_Su", "L0_ffn_Sd", "L0_ffn_Wsg"]
_OUTS = [((4, 512, 512), "float32")]


def kernel(**inputs):
    import numpy as _np
    import concourse.bacc as _bacc
    from concourse import mybir as _mybir
    from concourse.bass_utils import run_bass_kernel_spmd as _run

    nc = _bacc.Bacc("TRN2", target_bir_lowering=False, num_devices=1)
    arrays, args = {}, []
    for name in _INS:
        a = _np.ascontiguousarray(inputs[name])
        arrays[f"in_{name}_dram"] = a
        args.append(nc.dram_tensor(f"in_{name}_dram", a.shape, _mybir.dt.from_np(a.dtype), kind="ExternalInput").ap())
    for i, (shape, dtype) in enumerate(_OUTS):
        dt = _mybir.dt.from_np(_np.dtype(dtype))
        args.append(nc.dram_tensor(f"out_{i}_dram", shape, dt, kind="ExternalOutput").ap())
    decoder_kernel(nc, *args)
    r = _run(nc, [arrays], core_ids=[0])
    return r.results[0]["out_0_dram"]
```
